# Optimizing a Trainium2 kernel written in Bass

```python
import numpy as np
import jax
import jax.numpy as jnp

def _softmax(x, axis=-1):
    return jax.nn.softmax(x, axis=axis)

def _gelu(x):
    return jax.nn.gelu(x, approximate=True)

def _silu(x):
    return jax.nn.silu(x)

def _sigmoid(x):
    return jax.nn.sigmoid(x)

def _layernorm(x, axis=-1, eps=1e-05):
    m = jnp.mean(x, axis=axis, keepdims=True)
    v = jnp.var(x, axis=axis, keepdims=True)
    return (x - m) / jnp.sqrt(v + eps)

def _scatter_add(tgt, idx, src, axis=0):
    return tgt.at[idx].add(src)

def _segment_sum(src, seg, n):
    return jax.ops.segment_sum(src, seg, n)
kernel_name = 'mk_macaron_d2_jaxref_r8_ce9035'

def setup_inputs(seed: int=0):
    np.random.seed(seed)
    _w = jnp.asarray

    def _L0_attn_setup():
        import jax, jax.numpy as jnp
        from jax import lax
        import numpy as np
        import math
        EMBED_DIM = 128
        NUM_HEADS = 16
        REDUCTION = 2
        key = jax.random.key(seed)
        ks = jax.random.split(key, 11)
        B, N, C = (2, 512, EMBED_DIM)
        s = 1.0 / math.sqrt(C)
        return {'x': jax.random.normal(ks[0], (B, N, C), jnp.float32), 'q_w': jax.random.normal(ks[1], (C, C), jnp.float32) * s, 'q_b': jax.random.normal(ks[2], (C,), jnp.float32) * s, 'k_w': jax.random.normal(ks[3], (C, C), jnp.float32) * s, 'k_b': jax.random.normal(ks[4], (C,), jnp.float32) * s, 'v_w': jax.random.normal(ks[5], (C, C), jnp.float32) * s, 'v_b': jax.random.normal(ks[6], (C,), jnp.float32) * s, 'conv_w': jax.random.normal(ks[7], (C, 1, 3), jnp.float32) * 0.5, 'conv_b': jax.random.normal(ks[8], (C,), jnp.float32) * 0.1, 'out_w': jax.random.normal(ks[9], (C, C), jnp.float32) * s, 'out_b': jax.random.normal(ks[10], (C,), jnp.float32) * s}
    _L0_attn_in = _L0_attn_setup()

    def _L0_ffn_setup():
        import jax, jax.numpy as jnp
        import numpy as np
        E = 8
        TOP_K = 2
        B, S, D = (2, 512, 128)
        H = 512
        CAPACITY = 256

        def _moe(x, Wg, W1, b1, W2, b2):
            b, s, d = x.shape
            xf = x.reshape(b * s, d)
            logits = xf.astype(jnp.float32) @ Wg.astype(jnp.float32)
            probs = jax.nn.softmax(logits, axis=-1)
            vals, idx = jax.lax.top_k(probs, TOP_K)
            w = vals / (jnp.sum(vals, axis=-1, keepdims=True) + 1e-09)
            counts = jnp.zeros((E,), dtype=jnp.int32)
            combine = jnp.zeros((b * s, E), dtype=jnp.float32)
            for k in range(TOP_K):
                oh = jax.nn.one_hot(idx[:, k], E, dtype=jnp.int32)
                pos = jnp.cumsum(oh, axis=0) - 1 + counts[None, :]
                keep = (oh == 1) & (pos < CAPACITY)
                counts = counts + jnp.sum(keep.astype(jnp.int32), axis=0)
                combine = combine + w[:, k][:, None] * keep.astype(jnp.float32)
            out = jnp.zeros_like(xf)
            for e in range(E):
                h = jax.nn.gelu(xf @ W1[e] + b1[e])
                ye = h @ W2[e] + b2[e]
                out = out + combine[:, e][:, None].astype(xf.dtype) * ye
            return out.reshape(b, s, d)
        key = jax.random.key(seed)
        k0, k1, k2, k3 = jax.random.split(key, 4)
        return {'x': jax.random.normal(k0, (B, S, D), dtype=jnp.float32), 'Wg': jax.random.normal(k1, (D, E), dtype=jnp.float32) * 0.02, 'W1': jax.random.normal(k2, (E, D, H), dtype=jnp.float32) * 0.02, 'b1': jnp.zeros((E, H), dtype=jnp.float32), 'W2': jax.random.normal(k3, (E, H, D), dtype=jnp.float32) * 0.02, 'b2': jnp.zeros((E, D), dtype=jnp.float32)}
    _L0_ffn_in = _L0_ffn_setup()

    def _L1_attn_setup():
        import jax, jax.numpy as jnp
        import numpy as np
        EMBED_DIM = 128
        NUM_HEADS = 16
        HEAD_DIM = EMBED_DIM // NUM_HEADS

        def _mha(x, qkv_w, qkv_b, out_w, out_b):
            B, T, C = x.shape
            H, D = (NUM_HEADS, HEAD_DIM)
            qkv = x @ qkv_w.T + qkv_b
            q, k, v = jnp.split(qkv, 3, axis=-1)
            q = q.reshape(B, T, H, D).transpose(0, 2, 1, 3)
            k = k.reshape(B, T, H, D).transpose(0, 2, 1, 3)
            v = v.reshape(B, T, H, D).transpose(0, 2, 1, 3)
            att = jnp.einsum('bhqd,bhkd->bhqk', q, k) / np.sqrt(D)
            causal = jnp.tril(jnp.ones((T, T), dtype=bool))
            att = jnp.where(causal, att, -jnp.inf)
            att = jax.nn.softmax(att, axis=-1)
            out = jnp.einsum('bhqk,bhkd->bhqd', att, v)
            out = out.transpose(0, 2, 1, 3).reshape(B, T, C)
            return out @ out_w.T + out_b
        key = jax.random.key(seed)
        k1, k2, k3, k4, k5 = jax.random.split(key, 5)
        B, T, C = (2, 256, EMBED_DIM)
        s = 1.0 / np.sqrt(C)
        return {'x': jax.random.normal(k1, (B, T, C), dtype=jnp.float32), 'qkv_w': jax.random.uniform(k2, (3 * C, C), jnp.float32, -s, s), 'qkv_b': jax.random.uniform(k3, (3 * C,), jnp.float32, -s, s), 'out_w': jax.random.uniform(k4, (C, C), jnp.float32, -s, s), 'out_b': jax.random.uniform(k5, (C,), jnp.float32, -s, s)}
    _L1_attn_in = _L1_attn_setup()

    def _L1_ffn_setup():
        import math
        import jax, jax.numpy as jnp
        import numpy as np
        B, S, D, H, E, F = (2, 128, 128, 16, 16, 512)
        HEAD = D // H
        MOE_TOKEN_DROPOUT = 0.2
        EPS = 1e-05

        def layer_norm(x, w, b):
            mu = x.mean(-1, keepdims=True)
            var = ((x - mu) ** 2).mean(-1, keepdims=True)
            return (x - mu) * jax.lax.rsqrt(var + EPS) * w + b
        key = jax.random.key(seed)
        ks = jax.random.split(key, 16)
        w = lambda k, shape: jax.random.normal(k, shape, jnp.float32) * 0.02
        return {'hidden_states': jax.random.normal(ks[0], (B, S, D), jnp.float32), 'ln1_w': jnp.ones((D,), jnp.float32), 'ln1_b': jnp.zeros((D,), jnp.float32), 'q_w': w(ks[1], (D, D)), 'q_b': jnp.zeros((D,), jnp.float32), 'k_w': w(ks[2], (D, D)), 'k_b': jnp.zeros((D,), jnp.float32), 'v_w': w(ks[3], (D, D)), 'v_b': jnp.zeros((D,), jnp.float32), 'o_w': w(ks[4], (D, D)), 'o_b': jnp.zeros((D,), jnp.float32), 'ln2_w': jnp.ones((D,), jnp.float32), 'ln2_b': jnp.zeros((D,), jnp.float32), 'router_w': w(ks[5], (D, E)), 'fc1_w': w(ks[6], (E, D, F)), 'fc1_b': jnp.zeros((E, F), jnp.float32), 'fc2_w': w(ks[7], (E, F, D)), 'fc2_b': jnp.zeros((E, D), jnp.float32)}
    _L1_ffn_in = _L1_ffn_setup()
    _d = {'L0_attn_x': _L0_attn_in['x'], 'L0_attn_q_w': _L0_attn_in['q_w'], 'L0_attn_q_b': _L0_attn_in['q_b'], 'L0_attn_k_w': _L0_attn_in['k_w'], 'L0_attn_k_b': _L0_attn_in['k_b'], 'L0_attn_v_w': _L0_attn_in['v_w'], 'L0_attn_v_b': _L0_attn_in['v_b'], 'L0_attn_conv_w': _L0_attn_in['conv_w'], 'L0_attn_conv_b': _L0_attn_in['conv_b'], 'L0_attn_out_w': _L0_attn_in['out_w'], 'L0_attn_out_b': _L0_attn_in['out_b'], 'L0_ffn_Wg': _L0_ffn_in['Wg'], 'L0_ffn_W1': _L0_ffn_in['W1'], 'L0_ffn_b1': _L0_ffn_in['b1'], 'L0_ffn_W2': _L0_ffn_in['W2'], 'L0_ffn_b2': _L0_ffn_in['b2'], 'L1_attn_qkv_w': _L1_attn_in['qkv_w'], 'L1_attn_qkv_b': _L1_attn_in['qkv_b'], 'L1_attn_out_w': _L1_attn_in['out_w'], 'L1_attn_out_b': _L1_attn_in['out_b'], 'L1_ffn_ln1_w': _L1_ffn_in['ln1_w'], 'L1_ffn_ln1_b': _L1_ffn_in['ln1_b'], 'L1_ffn_q_w': _L1_ffn_in['q_w'], 'L1_ffn_q_b': _L1_ffn_in['q_b'], 'L1_ffn_k_w': _L1_ffn_in['k_w'], 'L1_ffn_k_b': _L1_ffn_in['k_b'], 'L1_ffn_v_w': _L1_ffn_in['v_w'], 'L1_ffn_v_b': _L1_ffn_in['v_b'], 'L1_ffn_o_w': _L1_ffn_in['o_w'], 'L1_ffn_o_b': _L1_ffn_in['o_b'], 'L1_ffn_ln2_w': _L1_ffn_in['ln2_w'], 'L1_ffn_ln2_b': _L1_ffn_in['ln2_b'], 'L1_ffn_router_w': _L1_ffn_in['router_w'], 'L1_ffn_fc1_w': _L1_ffn_in['fc1_w'], 'L1_ffn_fc1_b': _L1_ffn_in['fc1_b'], 'L1_ffn_fc2_w': _L1_ffn_in['fc2_w'], 'L1_ffn_fc2_b': _L1_ffn_in['fc2_b']}
    _x0 = _d['L0_attn_x']
    _d['L0_attn_x'] = jax.random.normal(jax.random.fold_in(jax.random.key(seed), 1), (8, 512, 128), dtype=_x0.dtype)
    del _x0
    return _d

def reference(L0_attn_x, L0_attn_q_w, L0_attn_q_b, L0_attn_k_w, L0_attn_k_b, L0_attn_v_w, L0_attn_v_b, L0_attn_conv_w, L0_attn_conv_b, L0_attn_out_w, L0_attn_out_b, L0_ffn_Wg, L0_ffn_W1, L0_ffn_b1, L0_ffn_W2, L0_ffn_b2, L1_attn_qkv_w, L1_attn_qkv_b, L1_attn_out_w, L1_attn_out_b, L1_ffn_ln1_w, L1_ffn_ln1_b, L1_ffn_q_w, L1_ffn_q_b, L1_ffn_k_w, L1_ffn_k_b, L1_ffn_v_w, L1_ffn_v_b, L1_ffn_o_w, L1_ffn_o_b, L1_ffn_ln2_w, L1_ffn_ln2_b, L1_ffn_router_w, L1_ffn_fc1_w, L1_ffn_fc1_b, L1_ffn_fc2_w, L1_ffn_fc2_b):

    def _L0_attn_ref(x, q_w, q_b, k_w, k_b, v_w, v_b, conv_w, conv_b, out_w, out_b):
        import jax, jax.numpy as jnp
        from jax import lax
        import numpy as np
        import math
        EMBED_DIM = 128
        NUM_HEADS = 16
        REDUCTION = 2
        B, N, C = x.shape
        H = NUM_HEADS
        D = C // H
        scale = 1.0 / math.sqrt(D)
        q = x @ q_w.T + q_b
        xd = jnp.transpose(x, (0, 2, 1))
        xd = lax.conv_general_dilated(xd, conv_w, window_strides=(REDUCTION,), padding=[(1, 1)], feature_group_count=C, dimension_numbers=('NCH', 'OIH', 'NCH'))
        xd = xd + conv_b[None, :, None]
        xd = jnp.transpose(xd, (0, 2, 1))
        k = xd @ k_w.T + k_b
        v = xd @ v_w.T + v_b
        Nk = k.shape[1]
        q = q.reshape(B, N, H, D).transpose(0, 2, 1, 3)
        k = k.reshape(B, Nk, H, D).transpose(0, 2, 1, 3)
        v = v.reshape(B, Nk, H, D).transpose(0, 2, 1, 3)
        att = jnp.einsum('bhnd,bhmd->bhnm', q, k) * scale
        att = jax.nn.softmax(att, axis=-1)
        out = jnp.einsum('bhnm,bhmd->bhnd', att, v)
        out = out.transpose(0, 2, 1, 3).reshape(B, N, C)
        return out @ out_w.T + out_b

    def _L0_ffn_ref(x, Wg, W1, b1, W2, b2):
        import jax, jax.numpy as jnp
        import numpy as np
        E = 8
        TOP_K = 2
        B, S, D = (2, 512, 128)
        H = 512
        CAPACITY = 256

        def _moe(x, Wg, W1, b1, W2, b2):
            b, s, d = x.shape
            xf = x.reshape(b * s, d)
            logits = xf.astype(jnp.float32) @ Wg.astype(jnp.float32)
            probs = jax.nn.softmax(logits, axis=-1)
            vals, idx = jax.lax.top_k(probs, TOP_K)
            w = vals / (jnp.sum(vals, axis=-1, keepdims=True) + 1e-09)
            counts = jnp.zeros((E,), dtype=jnp.int32)
            combine = jnp.zeros((b * s, E), dtype=jnp.float32)
            for k in range(TOP_K):
                oh = jax.nn.one_hot(idx[:, k], E, dtype=jnp.int32)
                pos = jnp.cumsum(oh, axis=0) - 1 + counts[None, :]
                keep = (oh == 1) & (pos < CAPACITY)
                counts = counts + jnp.sum(keep.astype(jnp.int32), axis=0)
                combine = combine + w[:, k][:, None] * keep.astype(jnp.float32)
            out = jnp.zeros_like(xf)
            for e in range(E):
                h = jax.nn.gelu(xf @ W1[e] + b1[e])
                ye = h @ W2[e] + b2[e]
                out = out + combine[:, e][:, None].astype(xf.dtype) * ye
            return out.reshape(b, s, d)
        return _moe(x, Wg, W1, b1, W2, b2)

    def _L1_attn_ref(x, qkv_w, qkv_b, out_w, out_b):
        import jax, jax.numpy as jnp
        import numpy as np
        EMBED_DIM = 128
        NUM_HEADS = 16
        HEAD_DIM = EMBED_DIM // NUM_HEADS

        def _mha(x, qkv_w, qkv_b, out_w, out_b):
            B, T, C = x.shape
            H, D = (NUM_HEADS, HEAD_DIM)
            qkv = x @ qkv_w.T + qkv_b
            q, k, v = jnp.split(qkv, 3, axis=-1)
            q = q.reshape(B, T, H, D).transpose(0, 2, 1, 3)
            k = k.reshape(B, T, H, D).transpose(0, 2, 1, 3)
            v = v.reshape(B, T, H, D).transpose(0, 2, 1, 3)
            att = jnp.einsum('bhqd,bhkd->bhqk', q, k) / np.sqrt(D)
            causal = jnp.tril(jnp.ones((T, T), dtype=bool))
            att = jnp.where(causal, att, -jnp.inf)
            att = jax.nn.softmax(att, axis=-1)
            out = jnp.einsum('bhqk,bhkd->bhqd', att, v)
            out = out.transpose(0, 2, 1, 3).reshape(B, T, C)
            return out @ out_w.T + out_b
        return _mha(x, qkv_w, qkv_b, out_w, out_b)

    def _L1_ffn_ref(hidden_states, ln1_w, ln1_b, q_w, q_b, k_w, k_b, v_w, v_b, o_w, o_b, ln2_w, ln2_b, router_w, fc1_w, fc1_b, fc2_w, fc2_b):
        import math
        import jax, jax.numpy as jnp
        import numpy as np
        B, S, D, H, E, F = (2, 128, 128, 16, 16, 512)
        HEAD = D // H
        MOE_TOKEN_DROPOUT = 0.2
        EPS = 1e-05

        def layer_norm(x, w, b):
            mu = x.mean(-1, keepdims=True)
            var = ((x - mu) ** 2).mean(-1, keepdims=True)
            return (x - mu) * jax.lax.rsqrt(var + EPS) * w + b
        b, s, _ = hidden_states.shape
        T = b * s
        neg = jnp.finfo(jnp.float32).min
        resid = hidden_states
        x = layer_norm(hidden_states, ln1_w, ln1_b)
        q = (x @ q_w + q_b) / math.sqrt(HEAD)
        k = x @ k_w + k_b
        v = x @ v_w + v_b
        split = lambda t: t.reshape(b, s, H, HEAD).transpose(0, 2, 1, 3)
        q, k, v = (split(q), split(k), split(v))
        scores = jnp.einsum('bhqd,bhkd->bhqk', q, k)
        causal = jnp.tril(jnp.ones((s, s), bool))
        scores = jnp.where(causal, scores, neg)
        attn = jax.nn.softmax(scores, axis=-1)
        ctx = jnp.einsum('bhqk,bhkd->bhqd', attn, v)
        ctx = ctx.transpose(0, 2, 1, 3).reshape(b, s, D)
        hidden = resid + (ctx @ o_w + o_b)
        resid = hidden
        xt = layer_norm(hidden, ln2_w, ln2_b).reshape(T, D)
        logits = xt @ router_w
        probs = jax.nn.softmax(logits, axis=-1)
        top1 = jnp.argmax(probs, axis=-1)
        m1 = jax.nn.one_hot(top1, E, dtype=jnp.float32)
        logits_no1 = jnp.where(m1 > 0, -jnp.inf, logits)
        top2 = jnp.argmax(logits_no1, axis=-1)
        m2 = jax.nn.one_hot(top2, E, dtype=jnp.float32)
        loc1 = jnp.cumsum(m1, axis=0) - 1.0
        loc2 = jnp.cumsum(m2, axis=0) - 1.0 + m1.sum(axis=0, keepdims=True)
        C = 2 * math.ceil(T / E)
        m1 = m1 * (loc1 < C)
        m2 = m2 * (loc2 < C)
        g1 = (probs * m1).sum(-1)
        g2 = (probs * m2).sum(-1)
        denom = jnp.maximum(g1 + g2, jnp.finfo(jnp.float32).eps)
        g1, g2 = (g1 / denom, g2 / denom)
        slot1 = (loc1 * m1).sum(-1).astype(jnp.int32)
        slot2 = (loc2 * m2).sum(-1).astype(jnp.int32)
        d1 = m1[:, :, None] * jax.nn.one_hot(slot1, C, dtype=jnp.float32)[:, None, :]
        d2 = m2[:, :, None] * jax.nn.one_hot(slot2, C, dtype=jnp.float32)[:, None, :]
        dispatch = d1 + d2
        combine = g1[:, None, None] * d1 + g2[:, None, None] * d2
        xin = jnp.einsum('tec,td->ecd', dispatch, xt)
        h = jnp.einsum('ecd,edf->ecf', xin, fc1_w) + fc1_b[:, None, :]
        h = jax.nn.gelu(h, approximate=False)
        eout = jnp.einsum('ecf,efd->ecd', h, fc2_w) + fc2_b[:, None, :]
        eout = eout * (1.0 - MOE_TOKEN_DROPOUT)
        moe_out = jnp.einsum('tec,ecd->td', combine, eout).reshape(b, s, D)
        return resid + moe_out
    x = L0_attn_x
    x = x + 0.5 * _L0_ffn_ref(_layernorm(x, axis=-1), L0_ffn_Wg, L0_ffn_W1, L0_ffn_b1, L0_ffn_W2, L0_ffn_b2)
    x = x + _L0_attn_ref(_layernorm(x, axis=-1), L0_attn_q_w, L0_attn_q_b, L0_attn_k_w, L0_attn_k_b, L0_attn_v_w, L0_attn_v_b, L0_attn_conv_w, L0_attn_conv_b, L0_attn_out_w, L0_attn_out_b)
    x = x + 0.5 * _L0_ffn_ref(_layernorm(x, axis=-1), L0_ffn_Wg, L0_ffn_W1, L0_ffn_b1, L0_ffn_W2, L0_ffn_b2)
    x = x + 0.5 * _L1_ffn_ref(_layernorm(x, axis=-1), L1_ffn_ln1_w, L1_ffn_ln1_b, L1_ffn_q_w, L1_ffn_q_b, L1_ffn_k_w, L1_ffn_k_b, L1_ffn_v_w, L1_ffn_v_b, L1_ffn_o_w, L1_ffn_o_b, L1_ffn_ln2_w, L1_ffn_ln2_b, L1_ffn_router_w, L1_ffn_fc1_w, L1_ffn_fc1_b, L1_ffn_fc2_w, L1_ffn_fc2_b)
    x = x + _L1_attn_ref(_layernorm(x, axis=-1), L1_attn_qkv_w, L1_attn_qkv_b, L1_attn_out_w, L1_attn_out_b)
    x = x + 0.5 * _L1_ffn_ref(_layernorm(x, axis=-1), L1_ffn_ln1_w, L1_ffn_ln1_b, L1_ffn_q_w, L1_ffn_q_b, L1_ffn_k_w, L1_ffn_k_b, L1_ffn_v_w, L1_ffn_v_b, L1_ffn_o_w, L1_ffn_o_b, L1_ffn_ln2_w, L1_ffn_ln2_b, L1_ffn_router_w, L1_ffn_fc1_w, L1_ffn_fc1_b, L1_ffn_fc2_w, L1_ffn_fc2_b)
    return x

_drawn_inputs = setup_inputs


def setup_inputs(seed=0):
    import zlib

    import numpy as np

    out = dict(_drawn_inputs(seed))
    spreads = {'L0_ffn_b1': (0.0, 0.8),
     'L0_ffn_b2': (0.0, 0.1),
     'L1_ffn_ln1_w': (1.0, 0.6),
     'L1_ffn_ln1_b': (0.0, 0.8),
     'L1_ffn_q_b': (0.0, 0.8),
     'L1_ffn_k_b': (0.0, 0.8),
     'L1_ffn_v_b': (0.0, 0.525),
     'L1_ffn_o_b': (0.0, 0.1),
     'L1_ffn_ln2_w': (1.0, 0.6),
     'L1_ffn_ln2_b': (0.0, 0.424),
     'L1_ffn_fc1_b': (0.0, 0.8),
     'L1_ffn_fc2_b': (0.0, 0.1)}
    factors = {'L0_attn_q_b': 5.357,
     'L0_attn_k_b': 8.0,
     'L0_ffn_W1': 2.976,
     'L0_ffn_W2': 2.696,
     'L1_ffn_q_w': 8.0,
     'L1_ffn_k_w': 8.0,
     'L1_ffn_v_w': 6.252,
     'L1_ffn_o_w': 3.328,
     'L1_ffn_fc1_w': 2.801}
    for name, (base, spread) in spreads.items():
        noise = np.random.default_rng([zlib.crc32(name.encode()), seed]).standard_normal(out[name].shape)
        drawn = base * np.exp(spread * noise) if base else spread * noise
        out[name] = jnp.asarray(drawn.astype(out[name].dtype))
    for name, factor in factors.items():
        out[name] = (out[name] * factor).astype(out[name].dtype)
    return out
```

```python
from contextlib import ExitStack

import concourse.bass as bass
from concourse import mybir

P = 128
F32 = mybir.dt.float32
BF16 = mybir.dt.bfloat16
I32 = mybir.dt.int32
ALU = mybir.AluOpType
ACT = mybir.ActivationFunctionType
AX = mybir.AxisListType

B, S, C = 8, 512, 128
T = B * S
NT = T // P
TB = S // P
H, D = 16, 8
G = 4
HG = H // G
SCORE_SCALE = float(D) ** -0.5
EPS = 1e-5
MASKED = -1e30
FH = 512
FC = FH // P

Q_PARTS = (0, 0, 1, 0, 2, 1)
K_PARTS = (0, 1, 0, 2, 0, 1)
NPROD = len(Q_PARTS)
ROWS = NPROD * D
MROW = 66
KMAX = MROW
KSC = MROW + 3

SC_BANK = 0
MX_BANK = 4
O_BANK = 6
MISC = 7
XT_BANK, H_BANK, Y_BANK = 0, 2, 6


class Signal:

    def __init__(self, handle):
        self.h, self.base = handle, 0

    def at(self, n):
        return self.h, n + self.base


def broadcast_rows(ap, n):
    return ap.unsqueeze(1).to_broadcast([P, n, ap.shape[1]])


def broadcast_last(ap, n):
    return ap.unsqueeze(2).to_broadcast([P, ap.shape[1], n])


def statistics(nc, k, dve, src, twice):
    s, half = k.sig, C // 2

    def tiles(b):
        for t in range(TB):
            ins = nc.vector.bn_stats(k.st[:, bass.ds(b * (TB * 6) + t * 6, 6)], src[:, bass.ds(b * S + t * P, P)])
        ins.then_inc(s.ln_stats.h, 1)

    tiles(0)
    with dve.Fori(1, B, 1) as b:
        tiles(b)
    dve.wait_ge(*s.ln_stats.at(B))
    st = k.st[:, :].rearrange("p (t n) -> p t n", n=6)
    mean, dev, both = k.mean[:, :], k.dev[:, :], k.rstd[:, :]
    nc.vector.tensor_tensor(mean, st[:, :, 1], st[:, :, 4], ALU.add)
    nc.vector.tensor_tensor(dev, st[:, :, 1], st[:, :, 4], ALU.subtract)
    nc.vector.tensor_tensor(both, st[:, :, 2], st[:, :, 5], ALU.add).then_inc(s.ln_step.h, 1)
    dve.wait_ge(*s.ln_step.at(1))
    nc.vector.tensor_scalar(mean, mean, 0.5, None, ALU.mult)
    nc.vector.tensor_tensor(dev, dev, dev, ALU.mult).then_inc(s.ln_step.h, 1)
    dve.wait_ge(*s.ln_step.at(2))
    nc.vector.scalar_tensor_tensor(dev, dev, half / 2.0, both, ALU.mult, ALU.add).then_inc(s.ln_var.h, 1)
    dve.wait_ge(*s.ln_std.at(1))
    nc.vector.reciprocal(k.rstd[:, :], k.std[:, :]).then_inc(s.ln_rstd.h, 1)
    dve.wait_ge(*s.ln_rstd.at(1))
    if twice:
        nc.vector.tensor_tensor(dev, dev, k.rstd[:, :], ALU.mult).then_inc(s.ln_step.h, 1)
        dve.wait_ge(*s.ln_step.at(3))
        nc.vector.tensor_tensor(dev, dev, k.rstd[:, :], ALU.mult).then_inc(s.ln_var.h, 1)
        dve.wait_ge(*s.ln_std.at(2))
        nc.vector.reciprocal(k.rstd2[:, :], k.std[:, :]).then_inc(s.ln_step.h, 1)
        dve.wait_ge(*s.ln_step.at(4))
        nc.vector.tensor_tensor(k.rstd2[:, :], k.rstd2[:, :], k.rstd[:, :], ALU.mult).then_inc(s.ln_rstd.h, 1)
        dve.wait_ge(*s.ln_rstd.at(2))


def deviations(nc, k, act, twice):
    s = k.sig
    for n in range(1 + twice):
        act.wait_ge(*s.ln_var.at(n + 1))
        nc.scalar.activation(k.std[:, :], k.dev[:, :], ACT.Sqrt, bias=k.eps[:, 0:1], scale=1.0 / C).then_inc(s.ln_std.h, 1)


def normalise(nc, k, src, b, scale, dst):
    for t in range(TB):
        ins = nc.vector.tensor_scalar(dst(t), src[:, bass.ds(b * S + t * P, P)], k.mean[:, bass.ds(b * TB + t, 1)],
                                      scale[:, bass.ds(b * TB + t, 1)], ALU.subtract, ALU.mult)
    return ins


def attention(nc, k, w, src, dst, causal, twice=False):
    s, PS = k.sig, k.PS
    conv = w.conv_w is not None
    nk = S // 2 if conv else S
    KB = nk // P
    if causal:
        chunks = [(0, (0, 1), 512), (0, (2, 3), 512), (1, (0, 1), 384), (1, (2, 3), 384),
                  (2, (0, 1, 2, 3), 256), (3, (0, 1, 2, 3), 128)]
        maxes = ([(0, (0, 1, 2, 3), 128)] + [(1, (2 * i, 2 * i + 1), 256) for i in range(2)]
                 + [(2, (i,), 384) for i in range(4)] + [(3, (i,), 512) for i in range(4)])
    else:
        chunks = [(kb, (2 * i, 2 * i + 1), 512) for kb in range(KB) for i in range(2)]
        maxes = [(qb, (2 * i, 2 * i + 1), nk) for qb in range(TB) for i in range(2)]
    NCH, NMX = len(chunks), len(maxes)
    at = [sum(len(c[1]) * c[2] for c in chunks[:i]) for i in range(NCH)]

    def sc_bank(c, i):
        _, heads, n = chunks[c]
        per = 512 // n if len(heads) > 2 else 1
        return SC_BANK + 2 * (c % 2) + i // per, (i % per) * n

    def order(first, last, g):
        has_prev = not (first and g == 0)
        has_max = not (last and g >= 2)
        proj = g == 0 and not last
        plan = []
        mx = [("max", i) for i in range(NMX)] if has_max else []
        take = -(-NMX // NCH)
        for c in range(NCH):
            plan.append(("score", c))
            if c == 0 and has_prev:
                plan.append(("value_p", KB - 1))
            if c == 1 and has_prev:
                plan.append(("o_out", 0))
            plan += mx[:take]
            mx = mx[take:]
            if c == 1 and proj:
                plan += [("norm", 0), ("x_T", 0)]
            if c == 2 and has_prev:
                plan.append(("o_T", 0))
            for kb in range(KB - 1):
                if c == max(i for i in range(NCH) if chunks[i][0] == kb) + 1:
                    plan.append(("value", kb))
            if c == 2 and proj:
                plan.append(("q", 0))
            if c == 3:
                if has_prev and g == 0:
                    plan.append(("ctx_T", 0))
                if proj:
                    plan.append(("k", 0))
                if has_prev and g == 0:
                    plan.append(("out", 0))
                if proj:
                    plan.append(("v", 0))
        plan += mx
        if has_max:
            plan.append(("max_T", 0))
        return plan

    def ahead(b, g):
        return (b, g + 2, 4 * b + g + 2) if g < 2 else (b + 1, g - 2, 4 * b + g + 2)

    with nc.Block() as block:

        @block.tensor
        def _(pe):
            misc = [None]

            def take_misc():
                if misc[0] is not None:
                    pe.wait_ge(*misc[0][0].at(misc[0][1]))

            def max_tile(bb, gg, u, t):
                qb, heads, n = maxes[t]
                if t == 0:
                    pe.wait_ge(*s.qk_landed[gg].at(32 * (bb + 1)))
                if not (isinstance(u, int) and u * NMX + t < 2):
                    pe.wait_ge(*s.max_taken.at(u * NMX + t - 1))
                bank = MX_BANK + (gg * NMX + t) % 2
                for i, h in enumerate(heads):
                    mm = pe.matmul(PS[:, bank, i * n:(i + 1) * n], k.qa[0:KMAX, gg, h, qb * P:(qb + 1) * P],
                                   k.ka[0:KMAX, gg, h, 0:n], start=True, stop=not causal)
                    if causal:
                        mm = pe.matmul(PS[:, bank, (i + 1) * n - P:(i + 1) * n], k.identb[:, :],
                                       k.mask_q[:, :], start=False, stop=True)
                mm.then_inc(s.max_full.h, 1)

            def max_transpose(bb, gg, u):
                pe.wait_ge(*s.max_taken.at((u + 1) * NMX))
                take_misc()
                pe.transpose(PS[0:16, MISC, 0:P], k.mx[:, gg % 2, :], k.ident[:, :]).then_inc(s.mT_full.h, 1)
                misc[0] = (s.mT_free, u + 1)

            def project(name, b1):
                if name == "x_T":
                    pe.wait_ge(*s.xa_ready.at(b1 + 1))
                    take_misc()
                    for t in range(TB):
                        mm = pe.transpose(PS[:, MISC, t * P:(t + 1) * P], k.xa[:, t, :], k.ident[:, :])
                    mm.then_inc(s.xT_full.h, 1)
                    misc[0] = (s.xT_free, b1 + 1)
                if name == "q":
                    take_misc()
                    pe.matmul(PS[:, MISC, :], w.wq, k.xnT[:, 1:S + 1], start=True, stop=True).then_inc(s.q_full.h, 1)
                    misc[0] = (s.q_free, b1 + 1)
                kv = k.xdT if conv else k.xnT[:, 1:S + 1]
                if name == "k":
                    if conv:
                        pe.wait_ge(*s.xd_ready.at(b1 + 1))
                    take_misc()
                    pe.matmul(PS[:, MISC, 0:nk], w.wk, kv[:, 0:nk], start=True, stop=True).then_inc(s.k_full.h, 1)
                    misc[0] = (s.k_free, b1 + 1)
                if name == "v":
                    take_misc()
                    for t in range(KB):
                        mm = pe.matmul(PS[:, MISC, t * P:(t + 1) * P], kv[:, t * P:(t + 1) * P], w.wv,
                                       start=True, stop=True)
                    mm.then_inc(s.v_full.h, 1)
                    misc[0] = (s.v_free, b1 + 1)

            def values(b, g, u, kb):
                if kb == 0:
                    pe.wait_ge(*s.vs_ready.at(u + 1))
                    if not (isinstance(u, int) and u < 1):
                        pe.wait_ge(*s.o_free.at(u))
                last = max(i for i in range(NCH) if chunks[i][0] == kb)
                pe.wait_ge(*s.pt_ready.at(u * NCH + last + 1))
                q0 = kb * P if causal else 0
                for c, (kk, heads, n) in enumerate(chunks):
                    if kk != kb:
                        continue
                    for i, h in enumerate(heads):
                        mm = pe.matmul(PS[32 * h:32 * h + 32, O_BANK, q0:S], k.vs[:, g, kb, h, :],
                                       k.pt[:, g % 2, at[c] + i * n:at[c] + (i + 1) * n],
                                       start=(kb == 0), stop=(kb == KB - 1))
                if kb == KB - 1:
                    mm.then_inc(s.pv_done.h, 1)

            def tail(name, b, g, u):
                if name == "o_T":
                    pe.wait_ge(*s.o_free.at(u + 1))
                    take_misc()
                    for q in range(TB):
                        mm = pe.transpose(PS[:, MISC, q * P:(q + 1) * P], k.osb[:, q * P:(q + 1) * P], k.ident[:, :])
                    mm.then_inc(s.oT_full.h, 1)
                    misc[0] = (s.oT_free, u + 1)
                if name == "ctx_T":
                    take_misc()
                    for q in range(TB):
                        mm = pe.transpose(PS[:, MISC, q * P:(q + 1) * P], k.ctx[:, q, :], k.ident[:, :])
                    mm.then_inc(s.cT_full.h, 1)
                    misc[0] = (s.cT_free, b + 1)
                if name == "out":
                    take_misc()
                    for q in range(TB):
                        mm = pe.matmul(PS[:, MISC, q * P:(q + 1) * P], k.ctxT[:, q * P:(q + 1) * P], w.wo,
                                       start=True, stop=True)
                    mm.then_inc(s.out_full.h, 1)
                    misc[0] = (s.out_free, b + 1)

            def score_chunk(b, g, u, c):
                kb, heads, n = chunks[c]
                if c == 0:
                    pe.wait_ge(*s.m_landed[g].at(48 * (b + 1)))
                if not (isinstance(u, int) and u * NCH + c < 2):
                    pe.wait_ge(*s.pt_ready.at(u * NCH + c - 1))
                q0 = kb * P if causal else 0
                for i, h in enumerate(heads):
                    bank, col = sc_bank(c, i)
                    mm = pe.matmul(PS[:, bank, col:col + n], k.ka[0:KSC, g, h, kb * P:(kb + 1) * P],
                                   k.qa[0:KSC, g, h, q0:S], start=True, stop=not causal)
                    if causal:
                        mm = pe.matmul(PS[:, bank, col:col + P], k.identb[:, :], k.mask_k[:, :],
                                       start=False, stop=True)
                mm.then_inc(s.sc_full.h, 1)

            def batch(b, first, last):
                misc[0] = (s.mT_free, 4 * b + 2)
                for g in range(G):
                    u = 4 * b + g
                    pb, pg = (b, g - 1) if g else (b - 1, G - 1)
                    for name, i in order(first, last, g):
                        if name == "score":
                            score_chunk(b, g, u, i)
                        elif name == "value":
                            values(b, g, u, i)
                        elif name == "value_p":
                            values(pb, pg, u - 1, i)
                        elif name == "max":
                            max_tile(*ahead(b, g), i)
                        elif name == "max_T":
                            max_transpose(*ahead(b, g))
                        elif name in ("x_T", "q", "k", "v"):
                            project(name, b + 1)
                        elif name in ("o_T", "ctx_T", "out"):
                            tail(name, pb, pg, u - 1)

            for name in ("x_T", "q", "k", "v"):
                project(name, 0)
            for g in range(2):
                for t in range(NMX):
                    max_tile(0, g, g, t)
                max_transpose(0, g, g)
            batch(0, True, False)
            with pe.Fori(1, B - 1, 1) as b:
                batch(b, False, False)
            batch(B - 1, False, True)
            values(B - 1, G - 1, 4 * B - 1, KB - 1)
            for name in ("o_T", "ctx_T", "out"):
                tail(name, B - 1, G - 1, 4 * B - 1)

        @block.scalar
        def _(act):
            def batch(b):
                for g in range(G):
                    u = 4 * b + g
                    for c, (kb, heads, n) in enumerate(chunks):
                        act.wait_ge(*s.sc_full.at(u * NCH + c + 1))
                        if c == 0 and not (isinstance(u, int) and u < 2):
                            act.wait_ge(*s.pv_done.at(u - 1))
                        b0 = SC_BANK + 2 * (c % 2)
                        nb = 1 if len(heads) * n <= 512 else 2
                        per = len(heads) // nb
                        scores = PS[:, b0:b0 + nb, 0:per * n]
                        probs = k.pt[:, g % 2, at[c]:at[c] + len(heads) * n].rearrange("p (b n) -> p b n", b=nb)
                        nc.scalar.activation(probs, scores, ACT.Exp, scale=SCORE_SCALE).then_inc(s.pt_ready.h, 1)

            deviations(nc, k, act, twice)
            batch(0)
            with act.Fori(1, B - 1, 1) as b:
                batch(b)
            batch(B - 1)

        @block.vector
        def _(dve):
            def norm(b):
                if not (isinstance(b, int) and b < 1):
                    dve.wait_ge(*s.xT_full.at(b))
                if twice:
                    normalise(nc, k, src, b, k.rstd, lambda t: dst[:, bass.ds(b * S + t * P, P)])
                normalise(nc, k, src, b, k.rstd2 if twice else k.rstd, lambda t: k.xa[:, t, :]).then_inc(s.xa_ready.h, 1)

            def project(name, b1):
                if name == "x_T":
                    dve.wait_ge(*s.xT_full.at(b1 + 1))
                    if w.ln_w is not None:
                        nc.vector.tensor_scalar(k.xnT[:, 1:S + 1], PS[:, MISC, :], w.ln_w, w.ln_b,
                                                ALU.mult, ALU.add).then_inc(s.xT_free.h, 1)
                    else:
                        nc.vector.tensor_copy(k.xnT[:, 1:S + 1], PS[:, MISC, :]).then_inc(s.xT_free.h, 1)
                    if conv:
                        dve.wait_ge(*s.xT_free.at(b1 + 1))
                        if not (isinstance(b1, int) and b1 < 1):
                            dve.wait_ge(*s.xd_ready.at(b1))
                        tap = lambda j: k.xnT[:, j:j + S].rearrange("p (t two) -> p t two", two=2)[:, :, 0]
                        nc.vector.tensor_scalar(k.cv[:, 0, :], tap(1), w.conv_w[:, 1:2], w.conv_b,
                                                ALU.mult, ALU.add).then_inc(s.cv_step.h, 1)
                        dve.wait_ge(*s.cv_step.at(2 * b1 + 1))
                        nc.vector.scalar_tensor_tensor(k.cv[:, 1, :], tap(0), w.conv_w[:, 0:1], k.cv[:, 0, :],
                                                       ALU.mult, ALU.add).then_inc(s.cv_step.h, 1)
                        dve.wait_ge(*s.cv_step.at(2 * b1 + 2))
                        nc.vector.scalar_tensor_tensor(k.xdT, tap(2), w.conv_w[:, 2:3], k.cv[:, 1, :],
                                                       ALU.mult, ALU.add).then_inc(s.xd_ready.h, 1)
                if name == "q":
                    dve.wait_ge(*s.q_full.at(b1 + 1))
                    if not (isinstance(b1, int) and b1 < 1):
                        dve.wait_ge(*s.pq_ready.at(2 * b1))
                    nc.vector.tensor_scalar(k.q32, PS[:, MISC, :], w.qb, None, ALU.add).then_inc(s.q_free.h, 1)
                if name == "k":
                    dve.wait_ge(*s.k_full.at(b1 + 1))
                    nc.vector.tensor_scalar(k.k32[:, 0:nk], PS[:, MISC, 0:nk], w.kb, None, ALU.add).then_inc(s.k_free.h, 1)
                if name == "v":
                    dve.wait_ge(*s.v_full.at(b1 + 1))
                    if not (isinstance(b1, int) and b1 < 1):
                        dve.wait_ge(*s.vs_ready.at(4 * b1))
                    nc.vector.tensor_tensor(k.vst[:, 0:KB, :], PS[:, MISC, 0:KB * P].rearrange("p (t c) -> p t c", c=P),
                                            broadcast_rows(w.vb, KB), ALU.add).then_inc(s.v_free.h, 1)

            def max_tile(bb, gg, u, t):
                qb, heads, n = maxes[t]
                dve.wait_ge(*s.max_full.at(u * NMX + t + 1))
                if t == 0 and not (isinstance(u, int) and u < 2):
                    dve.wait_ge(*s.mT_full.at(u - 1))
                bank = MX_BANK + (gg * NMX + t) % 2
                out = k.mx[:, gg % 2, :].rearrange("p (h q) -> p h q", q=TB)[:, heads[0]:heads[-1] + 1, qb]
                nc.vector.tensor_reduce(out, PS[:, bank, 0:len(heads) * n].rearrange("p (h n) -> p h n", n=n),
                                        AX.X, ALU.max).then_inc(s.max_taken.h, 1)

            def max_split(gg, u, used=None):
                dve.wait_ge(*s.mT_full.at(u + 1))
                if not (isinstance(u, int) and u < 1):
                    dve.wait_ge(*s.nm_ready.at(u))
                nc.vector.tensor_scalar(k.nm32[:, 0, :], PS[0:16, MISC, 0:P], -1.0, None, ALU.mult).then_inc(s.mT_free.h, 1)
                dve.wait_ge(*s.mT_free.at(u + 1))
                if used is not None:
                    dve.wait_ge(*s.m_landed[used[0]].at(used[1]))
                nc.vector.tensor_copy(k.nm[:, gg % 2, 0, :], k.nm32[:, 0, :]).then_inc(s.nm_step.h, 1)
                dve.wait_ge(*s.nm_step.at(3 * u + 1))
                nc.vector.tensor_tensor(k.nm32[:, 1, :], k.nm32[:, 0, :], k.nm[:, gg % 2, 0, :], ALU.subtract).then_inc(s.nm_step.h, 1)
                dve.wait_ge(*s.nm_step.at(3 * u + 2))
                nc.vector.tensor_copy(k.nm[:, gg % 2, 1, :], k.nm32[:, 1, :]).then_inc(s.nm_step.h, 1)
                dve.wait_ge(*s.nm_step.at(3 * u + 3))
                nc.vector.tensor_tensor(k.nm[:, gg % 2, 2, :], k.nm32[:, 1, :], k.nm[:, gg % 2, 1, :], ALU.subtract).then_inc(s.nm_ready.h, 1)

            def tail(name, b, g, u):
                if name == "o_out":
                    dve.wait_ge(*s.pv_done.at(u + 1))
                    if not (isinstance(u, int) and u < 1):
                        dve.wait_ge(*s.oT_full.at(u))
                    nc.vector.tensor_copy(k.osb, PS[:, O_BANK, :]).then_inc(s.o_free.h, 1)
                if name == "o_T":
                    dve.wait_ge(*s.oT_full.at(u + 1))
                    o_T = PS[:, MISC, :].rearrange("p (q h c) -> p q h c", q=TB, h=HG)
                    nc.vector.reciprocal(k.rec[:, :, :], o_T[:, :, :, D]).then_inc(s.rec_done.h, 1)
                    dve.wait_ge(*s.rec_done.at(u + 1))
                    if g == 0 and not (isinstance(b, int) and b < 1):
                        dve.wait_ge(*s.cT_full.at(b))
                    nc.vector.tensor_tensor(k.ctx[:, :, g * 32:g * 32 + 32].rearrange("p q (h d) -> p q h d", h=HG),
                                            o_T[:, :, :, 0:D], k.rec[:, :, :].unsqueeze(3).to_broadcast([P, TB, HG, D]),
                                            ALU.mult).then_inc(s.oT_free.h, 1)
                if name == "ctx_T":
                    dve.wait_ge(*s.cT_full.at(b + 1))
                    nc.vector.tensor_copy(k.ctxT, PS[:, MISC, :]).then_inc(s.cT_free.h, 1)
                if name == "out":
                    dve.wait_ge(*s.out_full.at(b + 1))
                    if not (isinstance(b, int) and b < 1):
                        dve.wait_ge(*s.res_done.at(b))
                    nc.vector.tensor_tensor(k.tmp[:, :, :], PS[:, MISC, :].rearrange("p (q c) -> p q c", c=P),
                                            broadcast_rows(w.ob, TB), ALU.add).then_inc(s.out_free.h, 1)
                    dve.wait_ge(*s.out_free.at(b + 1))
                    dve.wait_ge(*s.xa_ready.at(b + 1))
                    residual = dst if twice else src
                    nc.vector.tensor_tensor(dst[:, bass.ds(b * S, S)], residual[:, bass.ds(b * S, S)],
                                            k.tmp[:, :, :].rearrange("p q c -> p (q c)"), ALU.add).then_inc(s.res_done.h, 1)

            def batch(b, first, last):
                for g in range(G):
                    u = 4 * b + g
                    pb, pg = (b, g - 1) if g else (b - 1, G - 1)
                    for name, i in order(first, last, g):
                        if name == "norm":
                            norm(b + 1)
                        elif name in ("x_T", "q", "k", "v"):
                            project(name, b + 1)
                        elif name == "max":
                            max_tile(*ahead(b, g), i)
                        elif name == "max_T":
                            bb, gg, uu = ahead(b, g)
                            max_split(gg, uu, used=(g, 48 * (b + 1)))
                        elif name in ("o_out", "o_T", "ctx_T", "out"):
                            tail(name, pb, pg, u - 1)

            statistics(nc, k, dve, src, twice)
            norm(0)
            for name in ("x_T", "q", "k", "v"):
                project(name, 0)
            for g in range(2):
                for t in range(NMX):
                    max_tile(0, g, g, t)
                max_split(g, g)
            batch(0, True, False)
            with dve.Fori(1, B - 1, 1) as b:
                batch(b, False, False)
            batch(B - 1, False, True)
            for name in ("o_out", "o_T", "ctx_T", "out"):
                tail(name, B - 1, G - 1, 4 * B - 1)

        @block.gpsimd
        def _(pool):
            def split(side, b):
                full, n = (k.q32, S) if side == 0 else (k.k32[:, 0:nk], nk)
                pool.wait_ge(*(s.q_free if side == 0 else s.k_free).at(b + 1))
                if side == 0 and not (isinstance(b, int) and b < 1):
                    pool.wait_ge(*s.parts_written.at(16 * 2 * NPROD * b))
                hi, mid, lo = (k.parts[:, side, j, 0:n] for j in range(3))
                pool.tensor_copy(hi, full).then_inc(s.sp_hi.h, 1)
                pool.wait_ge(*s.sp_hi.at(2 * b + side + 1))
                pool.tensor_tensor(k.rest[:, 0:n], full, hi, ALU.subtract).then_inc(s.sp_rest.h, 1)
                pool.wait_ge(*s.sp_rest.at(2 * b + side + 1))
                pool.tensor_copy(mid, k.rest[:, 0:n]).then_inc(s.sp_mid.h, 1)
                pool.wait_ge(*s.sp_mid.at(2 * b + side + 1))
                pool.tensor_tensor(lo, k.rest[:, 0:n], mid, ALU.subtract).then_inc(s.pq_ready.h, 1)
                pool.wait_ge(*s.pq_ready.at(2 * b + side + 1))

            def spread(b, g):
                if g == 0:
                    pool.wait_ge(*s.v_free.at(b + 1))
                if not (isinstance(b, int) and b < 1):
                    pool.wait_ge(*s.pv_done.at(4 * b - 3 + g))
                pool.tensor_copy(k.vs[:, g, 0:KB, :, 0:D], k.vst[:, 0:KB, g * 32:g * 32 + 32]
                                 .rearrange("p t (h d) -> p t h d", h=HG)).then_inc(s.vs_ready.h, 1)

            def batch(b):
                split(0, b)
                split(1, b)
                for g in range(G):
                    spread(b, g)

            for b in range(B):
                batch(b)

        @block.sync
        def _(sp):
            def write_parts(b):
                if not (isinstance(b, int) and b < 1):
                    for g in range(G):
                        sp.wait_ge(*s.qk_landed[g].at(32 * b))
                for side, parts, n, scratch in ((0, Q_PARTS, S, k.q_dram), (1, K_PARTS, nk, k.k_dram)):
                    sp.wait_ge(*s.pq_ready.at(2 * b + side + 1))
                    for r, part in enumerate(parts):
                        sp.dma_start(scratch[r, :, :, 0:n].rearrange("d h t -> h d t"),
                                     k.parts[:, side, part, 0:n]).then_inc(s.parts_written.h, 16)

            def load(b, g):
                sp.wait_ge(*s.parts_written.at(16 * 2 * NPROD * (b + 1)))
                if not (isinstance(b, int) and b < 1):
                    sp.wait_ge(*s.sc_full.at((4 * b - 3 + g) * NCH))
                for arr, scratch, n in ((k.qa, k.q_dram, S), (k.ka, k.k_dram, nk)):
                    sp.dma_start(arr[0:ROWS, g, :, 0:n], scratch[:, :, g * HG:(g + 1) * HG, 0:n]
                                 .rearrange("r d h t -> (r d) h t")).then_inc(s.qk_landed[g].h, 16)

            def put_max(b, g):
                u = 4 * b + g
                sp.wait_ge(*s.nm_ready.at(u + 1))
                for j in range(3):
                    sp.dma_start(k.qa[MROW + j:MROW + j + 1, g, :, :].rearrange("o h (q t) -> o (h q) t", t=P),
                                 k.nm[:, g % 2, j, :]).then_inc(s.m_landed[g].h, 16)

            def batch(b, last):
                if not last:
                    write_parts(b + 1)
                put_max(b, 2)
                if not last:
                    load(b + 1, 0)
                put_max(b, 3)
                if not last:
                    load(b + 1, 1)
                    put_max(b + 1, 0)
                    load(b + 1, 2)
                    put_max(b + 1, 1)
                    load(b + 1, 3)

            write_parts(0)
            for g in range(G):
                load(0, g)
            put_max(0, 0)
            put_max(0, 1)
            for b in range(B):
                batch(b, b == B - 1)

    U = 4 * B
    counts = {
        s.ln_stats: B, s.ln_step: 2 + 2 * twice, s.ln_var: 1 + twice, s.ln_std: 1 + twice,
        s.ln_rstd: 1 + twice, s.xa_ready: B, s.xT_full: B, s.xT_free: B, s.q_full: B,
        s.q_free: B, s.k_full: B, s.k_free: B, s.v_full: B, s.v_free: B, s.cT_full: B, s.cT_free: B,
        s.out_full: B, s.out_free: B, s.res_done: B, s.max_full: U * NMX, s.max_taken: U * NMX,
        s.mT_full: U, s.mT_free: U, s.nm_step: 3 * U, s.nm_ready: U, s.pv_done: U, s.o_free: U, s.oT_full: U,
        s.oT_free: U, s.rec_done: U, s.vs_ready: U, s.sc_full: U * NCH, s.pt_ready: U * NCH,
        s.sp_hi: 2 * B, s.sp_rest: 2 * B, s.sp_mid: 2 * B, s.pq_ready: 2 * B, s.parts_written: 16 * 2 * NPROD * B,
    }
    if conv:
        counts |= {s.cv_step: 2 * B, s.xd_ready: B}
    counts |= {x: 32 * B for x in s.qk_landed} | {x: 48 * B for x in s.m_landed}
    for signal, n in counts.items():
        signal.base += n


def moe(nc, k, w, src, dst, E, capacity, gate_scale, renorm, src_scale):
    s, PS = k.sig, k.PS
    ST = capacity // P
    NE = NT * E
    PAIRS = E // 2
    FAR = 1 << 16
    GELU = ACT.Gelu_apprx_tanh if w.gelu_tanh else ACT.Gelu
    NG = NT // TB

    def over_e(ap):
        return ap.unsqueeze(2).to_broadcast([P, NT, E])

    def all_pairs(eng, pair):
        pair(0, False)
        with eng.Fori(1, PAIRS - 1, 1) as j:
            pair(j, False)
        pair(PAIRS - 1, True)

    with nc.Block() as block:

        @block.tensor
        def _(pe):
            def route(i):
                pe.wait_ge(*s.gx_ready.at(i + 1))
                if not (isinstance(i, int) and i < 1):
                    pe.wait_ge(*s.gT_free.at(i))
                for t in range(TB):
                    mm = pe.transpose(PS[:, 0, t * P:(t + 1) * P], k.xa[:, t, :], k.ident[:, :])
                mm.then_inc(s.gT_full.h, 1)
                pe.wait_ge(*s.gT_free.at(i + 1))
                if not (isinstance(i, int) and i < 1):
                    pe.wait_ge(*s.gl_free.at(i))
                for t in range(TB):
                    mm = pe.matmul(PS[:, 1, t * E:(t + 1) * E], k.xnT[:, 1 + t * P:1 + (t + 1) * P], w.wg,
                                   start=True, stop=True)
                mm.then_inc(s.gl_full.h, 1)

            route(0)
            with pe.Fori(1, NG, 1) as i:
                route(i)
            for c in range(2):
                pe.wait_ge(*s.choice_ready.at(c + 1))
                oh = k.onehot[:, c, 0:NE]
                pe.matmul(PS[:, 2 + 2 * c, 0:NE], k.tri[:, :], oh, start=True, stop=True)
                pe.matmul(PS[:, 3 + 2 * c, 0:NE], k.onesb[:, :], oh, start=True, stop=True).then_inc(s.rank_full.h, 1)
            pe.wait_ge(*s.idx_ready.at(1))

            def rows_T(j, par):
                e = 2 * j + par
                pe.wait_ge(*s.xe_landed[par].at(16 * (j + 1)))
                if not (isinstance(j, int) and j < 1):
                    pe.wait_ge(*s.eT_free.at(e - 1))
                for t in range(ST):
                    mm = pe.transpose(PS[:, XT_BANK + par, t * P:(t + 1) * P], k.xe[:, par, t, :], k.ident[:, :])
                mm.then_inc(s.eT_full.h, 1)

            def hidden(j, par):
                e = 2 * j + par
                pe.wait_ge(*s.eT_free.at(e + 1))
                pe.wait_ge(*s.w1_landed[par].at(16 * (j + 1)))
                for f in range(FC):
                    if not (isinstance(j, int) and e < 1):
                        pe.wait_ge(*s.act_done.at(e * FC - FC + f + 1))
                    pe.matmul(PS[:, H_BANK + f, 0:capacity], k.w1[:, par, f * P:(f + 1) * P],
                              k.xeT[:, par, 0:capacity], start=True, stop=True).then_inc(s.h_full.h, 1)

            def output(j, par):
                e = 2 * j + par
                pe.wait_ge(*s.w2_landed[par].at(16 * (j + 1)))
                pe.wait_ge(*s.act_done.at(e * FC + FC))
                if not (isinstance(j, int) and j < 1):
                    pe.wait_ge(*s.y_ready.at(e - 1))
                for t in range(ST):
                    for f in range(FC):
                        mm = pe.matmul(PS[:, Y_BANK + par, t * P:(t + 1) * P], k.hT[:, par, f, t * P:(t + 1) * P],
                                       k.w2[:, par, f, :], start=(f == 0), stop=(f == FC - 1))
                mm.then_inc(s.y_full.h, 1)

            def pair(j, last):
                hidden(j, 0)
                rows_T(j, 1)
                output(j, 0)
                hidden(j, 1)
                if not last:
                    rows_T(j + 1, 0)
                output(j, 1)

            rows_T(0, 0)
            all_pairs(pe, pair)

        @block.scalar
        def _(act):
            def route(i):
                act.wait_ge(*s.gT_full.at(i + 1))
                nc.scalar.activation(k.xnT[:, 1:S + 1], PS[:, 0, :], ACT.Copy).then_inc(s.gT_free.h, 1)
                act.wait_ge(*s.gl_full.at(i + 1))
                nc.scalar.activation(k.logits[:, bass.ds(i * (TB * E), TB * E)], PS[:, 1, 0:TB * E],
                                     ACT.Copy).then_inc(s.gl_free.h, 1)

            deviations(nc, k, act, False)
            route(0)
            with act.Fori(1, NG, 1) as i:
                route(i)
            act.wait_ge(*s.diff_ready.at(1))
            nc.scalar.activation(k.ra[:, 0:NE], k.ra[:, 0:NE], ACT.Exp).then_inc(s.exp_ready.h, 1)
            act.wait_ge(*s.diff_ready.at(2))
            nc.scalar.activation(k.rv[:, 6, :], k.rv[:, 6, :], ACT.Exp).then_inc(s.exp_ready.h, 1)

            def pair(j, last):
                for par in range(2):
                    e = 2 * j + par
                    for f in range(FC):
                        act.wait_ge(*s.h_full.at(e * FC + f + 1))
                        if f == 0 and not (isinstance(j, int) and j < 1):
                            act.wait_ge(*s.y_full.at(e - 1))
                        nc.scalar.activation(k.hT[:, par, f, 0:capacity], PS[:, H_BANK + f, 0:capacity], GELU,
                                             bias=w.b1[:, bass.ds(e * FC + f, 1)]).then_inc(s.act_done.h, 1)

            all_pairs(act, pair)

        @block.vector
        def _(dve):
            affine = w.ln_w is not None

            def norm(i):
                if not (isinstance(i, int) and i < 1):
                    dve.wait_ge(*s.gT_full.at(i))
                    dve.wait_ge(*s.kept.at(i))
                ins = normalise(nc, k, src, i, k.rstd, lambda t: k.xa[:, t, :])
                if affine:
                    ins.then_inc(s.ga_step.h, 1)
                    dve.wait_ge(*s.ga_step.at(2 * i + 1))
                    nc.vector.tensor_tensor(k.xa[:, :, :], k.xa[:, :, :], broadcast_rows(w.ln_w, TB), ALU.mult)\
                        .then_inc(s.ga_step.h, 1)
                    dve.wait_ge(*s.ga_step.at(2 * i + 2))
                    ins = nc.vector.tensor_tensor(k.xa[:, :, :], k.xa[:, :, :], broadcast_rows(w.ln_b, TB), ALU.add)
                ins.then_inc(s.gx_ready.h, 1)

            statistics(nc, k, dve, src, False)
            norm(0)
            with dve.Fori(1, NG, 1) as i:
                norm(i)

            steps = [0]

            def link(ins):
                ins.then_inc(s.rt_step.h, 1)
                steps[0] += 1
                dve.wait_ge(*s.rt_step.at(steps[0]))

            v = lambda n: k.rv[:, n, :]
            e3 = lambda tile: tile[:, 0:NE].rearrange("p (t e) -> p t e", e=E)
            logits, ra, rb, rc, rd = e3(k.logits), e3(k.ra), e3(k.rb), e3(k.rc), e3(k.rd)
            onehot = [k.onehot[:, c, 0:NE].rearrange("p (t e) -> p t e", e=E) for c in range(2)]
            tt, red = nc.vector.tensor_tensor, nc.vector.tensor_reduce
            TOP, LAST = (0, 1), (2, 3)

            def choose(c, values):
                link(red(v(TOP[c]), values, AX.X, ALU.max))
                link(tt(rb, values, over_e(v(TOP[c])), ALU.is_equal))
                link(tt(rb, rb, broadcast_rows(w.down, NT), ALU.mult))
                link(red(v(LAST[c]), rb, AX.X, ALU.max))
                tt(onehot[c], rb, over_e(v(LAST[c])), ALU.is_equal).then_inc(s.choice_ready.h, 1)
                dve.wait_ge(*s.choice_ready.at(c + 1))

            dve.wait_ge(*s.gl_free.at(NG))
            choose(0, logits)
            tt(ra, logits, over_e(v(TOP[0])), ALU.subtract).then_inc(s.diff_ready.h, 1)
            link(nc.vector.scalar_tensor_tensor(rc, onehot[0], MASKED, logits, ALU.mult, ALU.add))
            choose(1, rc)
            tt(v(6), v(TOP[1]), v(TOP[0]), ALU.subtract).then_inc(s.diff_ready.h, 1)
            dve.wait_ge(*s.exp_ready.at(1))
            link(red(v(4), ra, AX.X, ALU.add))
            link(nc.vector.reciprocal(v(4), v(4)))
            dve.wait_ge(*s.exp_ready.at(2))
            link(tt(v(5), v(6), v(4), ALU.mult))

            for c in range(2):
                dve.wait_ge(*s.rank_full.at(c + 1))
                within = PS[:, 2 + 2 * c, 0:NE].rearrange("p (t e) -> p t e", e=E)
                total = PS[:, 3 + 2 * c, 0:NE].rearrange("p (t e) -> p t e", e=E)
                upto = (rc, rd)[c]
                for e in range(E):
                    ins = nc.vector.tensor_tensor_scan(upto[:, :, e], k.ones_t[:, :], total[:, :, e], 0.0, ALU.mult, ALU.add)
                link(ins)
                link(tt(rb, upto, total, ALU.subtract))
                link(tt(rb, rb, within, ALU.add))
                if c == 1:
                    link(nc.vector.tensor_scalar(k.before[:, 0:E], rc[:, NT - 1, :], float(w.counted), None, ALU.min))
                    link(tt(rb, rb, broadcast_rows(k.before[:, 0:E], NT), ALU.add))
                link(tt(rb, rb, onehot[c], ALU.mult))
                link(red(v(7), rb, AX.X, ALU.add))
                link(nc.vector.tensor_scalar(v(8 + c), v(7), float(capacity), None, ALU.is_lt))
                link(nc.vector.tensor_scalar(v(6), v(LAST[c]), -float(capacity), float(E * capacity), ALU.mult, ALU.add))
                link(tt(v(6), v(6), v(7), ALU.add))
                link(nc.vector.scalar_tensor_tensor(v(7), v(8 + c), -float(FAR), v(6), ALU.mult, ALU.add))
                link(nc.vector.tensor_scalar(k.idx[:, c, :], v(7), float(FAR), None, ALU.add))
                link(tt(k.idx[:, 2 + c, :], v(6), v(8 + c), ALU.mult))
            nc.vector.tensor_copy(v(7), v(8)).then_inc(s.idx_ready.h, 1)
            dve.wait_ge(*s.idx_ready.at(1))

            if renorm[0] == "add":
                link(tt(v(6), v(4), v(5), ALU.add))
                link(nc.vector.tensor_scalar(v(6), v(6), renorm[1], None, ALU.add))
            for c in range(2):
                link(tt(v(4 + c), v(4 + c), v(8 + c), ALU.mult))
            if renorm[0] == "max":
                link(tt(v(6), v(4), v(5), ALU.add))
                link(nc.vector.tensor_scalar(v(6), v(6), renorm[1], None, ALU.max))
            link(nc.vector.reciprocal(v(6), v(6)))
            for c in range(2):
                link(nc.vector.scalar_tensor_tensor(v(4 + c), v(4 + c), gate_scale, v(6), ALU.mult, ALU.mult))
            if src_scale:
                for i in range(NG):
                    ins = nc.vector.scalar_tensor_tensor(dst[:, i * S:(i + 1) * S], src[:, i * S:(i + 1) * S], src_scale,
                                                         dst[:, i * S:(i + 1) * S], ALU.mult, ALU.add)
                link(ins)
            k.route_steps = steps[0]

            def rows(j, par):
                e = 2 * j + par
                dve.wait_ge(*s.eT_full.at(e + 1))
                if not (isinstance(j, int) and j < 1):
                    dve.wait_ge(*s.h_full.at((e - 1) * FC))
                nc.vector.tensor_copy(k.xeT[:, par, 0:capacity], PS[:, XT_BANK + par, 0:capacity]).then_inc(s.eT_free.h, 1)

            def result(j, par):
                e = 2 * j + par
                dve.wait_ge(*s.y_full.at(e + 1))
                if not (isinstance(j, int) and j < 1):
                    dve.wait_ge(*s.y_stored[par].at(16 * j))
                b2 = w.b2[:, bass.ds(e * C, C)].unsqueeze(1).to_broadcast([P, ST, C])
                nc.vector.tensor_tensor(k.ys[:, par, 0:ST, :], PS[:, Y_BANK + par, 0:capacity]
                                        .rearrange("p (t c) -> p t c", c=C), b2, ALU.add).then_inc(s.y_ready.h, 1)

            def pair(j, last):
                rows(j, 1)
                result(j, 0)
                if not last:
                    rows(j + 1, 0)
                result(j, 1)

            rows(0, 0)
            all_pairs(dve, pair)

            for i in range(NG):
                dve.wait_ge(*s.gathered[i].at(16 * 2 * TB))
                for c in range(2):
                    for t in range(i * TB, (i + 1) * TB):
                        ins = nc.vector.scalar_tensor_tensor(dst[:, t * P:(t + 1) * P], k.rows_back[:, c, t, :],
                                                             k.rv[:, 4 + c, t:t + 1], dst[:, t * P:(t + 1) * P],
                                                             ALU.mult, ALU.add)
                    ins.then_inc(s.combined.h, 1)
                    dve.wait_ge(*s.combined.at(2 * i + c + 1))

        @block.gpsimd
        def _(pool):
            def keep(i):
                pool.wait_ge(*s.gx_ready.at(i + 1))
                pool.tensor_copy(k.xn[:, i * S:(i + 1) * S], k.xa[:, :, :].rearrange("p t c -> p (t c)")).then_inc(s.kept.h, 1)

            for i in range(NG):
                keep(i)
            pool.wait_ge(*s.kept.at(NG))
            pool.wait_ge(*s.idx_ready.at(1))
            for t in range(NT):
                for c in range(2):
                    pool.indirect_dma_start(k.x_slots[0:E * capacity, :], bass.IndirectOffsetOnAxis(k.idx[:, c, t:t + 1], 0),
                                            k.xn[:, t * P:(t + 1) * P], None, bounds_check=E * capacity - 1,
                                            oob_is_err=False).then_inc(s.scattered.h, 16)
            for par in range(2):
                pool.wait_ge(*s.y_stored[par].at(16 * PAIRS))
            for t in range(NT):
                for c in range(2):
                    pool.indirect_dma_start(k.rows_back[:, c, t, :], None, k.y_slots[0:E * capacity, :],
                                            bass.IndirectOffsetOnAxis(k.idx[:, 2 + c, t:t + 1], 0),
                                            bounds_check=E * capacity - 1, oob_is_err=False)\
                        .then_inc(s.gathered[t // TB].h, 16)

        @block.sync
        def _(sp):
            def load_weights(j, par):
                e = 2 * j + par
                if not (isinstance(j, int) and j < 1):
                    sp.wait_ge(*s.y_full.at(e - 1))
                sp.dma_start(k.w1[:, par, :], w.w1[bass.ds(e * C, C), :]).then_inc(s.w1_landed[par].h, 16)
                sp.dma_start(k.w2[:, par, :, :], w.w2[bass.ds(e * FH, FH), :].rearrange("(f p) c -> p f c", p=P))\
                    .then_inc(s.w2_landed[par].h, 16)

            def load_rows(j, par):
                e = 2 * j + par
                sp.dma_start(k.xe[:, par, 0:ST, :], k.x_slots[bass.ds(e * capacity, capacity), :]
                             .rearrange("(t p) c -> p t c", p=P)).then_inc(s.xe_landed[par].h, 16)

            def store(j, par):
                e = 2 * j + par
                sp.wait_ge(*s.y_ready.at(e + 1))
                sp.dma_start(k.y_slots[bass.ds(e * capacity, capacity), :].rearrange("(t p) c -> p t c", p=P),
                             k.ys[:, par, 0:ST, :]).then_inc(s.y_stored[par].h, 16)

            def pair(j, last):
                for par in range(2):
                    store(j, par)
                    if not last:
                        load_weights(j + 1, par)
                        load_rows(j + 1, par)

            for par in range(2):
                load_weights(0, par)
            sp.wait_ge(*s.scattered.at(16 * 2 * NT))
            for par in range(2):
                load_rows(0, par)
            for j in range(PAIRS):
                pair(j, j == PAIRS - 1)

    counts = {
        s.ln_stats: B, s.ln_step: 2, s.ln_var: 1, s.ln_std: 1, s.ln_rstd: 1, s.gx_ready: NG, s.gT_full: NG, s.gT_free: NG, s.gl_full: NG,
        s.gl_free: NG, s.kept: NG, s.choice_ready: 2, s.diff_ready: 2, s.exp_ready: 2, s.rank_full: 2,
        s.rt_step: k.route_steps, s.idx_ready: 1, s.scattered: 16 * 2 * NT, s.eT_full: E, s.eT_free: E,
        s.h_full: FC * E, s.act_done: FC * E, s.y_full: E, s.y_ready: E, s.combined: 2 * NG,
    }
    if w.ln_w is not None:
        counts[s.ga_step] = 2 * NG
    for group in (s.xe_landed, s.w1_landed, s.w2_landed, s.y_stored):
        counts |= {x: 16 * PAIRS for x in group}
    counts |= {x: 16 * 2 * TB for x in s.gathered}
    for signal, n in counts.items():
        signal.base += n


class Signals:

    def __init__(self, new):
        self.ln_stats = new("ln_stats")
        self.ln_step = new("ln_step")
        self.ln_var = new("ln_var")
        self.ln_std = new("ln_std")
        self.ln_rstd = new("ln_rstd")
        self.xa_ready = new("xa_ready")
        self.xT_full, self.xT_free = new("xT_full"), new("xT_free")
        self.q_full, self.q_free = new("q_full"), new("q_free")
        self.k_full, self.k_free = new("k_full"), new("k_free")
        self.v_full, self.v_free = new("v_full"), new("v_free")
        self.cT_full, self.cT_free = new("cT_full"), new("cT_free")
        self.out_full, self.out_free = new("out_full"), new("out_free")
        self.res_done = new("res_done")
        self.cv_step = new("cv_step")
        self.xd_ready = new("xd_ready")
        self.sp_hi, self.sp_rest, self.sp_mid = new("sp_hi"), new("sp_rest"), new("sp_mid")
        self.pq_ready = new("pq_ready")
        self.parts_written = new("parts_written")
        self.mT_full, self.mT_free = new("mT_full"), new("mT_free")
        self.oT_full, self.oT_free = new("oT_full"), new("oT_free")
        self.nm_step = new("nm_step")
        self.nm_ready = new("nm_ready")
        self.pv_done = new("pv_done")
        self.o_free = new("o_free")
        self.rec_done = new("rec_done")
        self.vs_ready = new("vs_ready")
        self.qk_landed = [new(f"qk_landed{g}") for g in range(G)]
        self.m_landed = [new(f"m_landed{g}") for g in range(G)]
        self.max_full, self.max_taken = new("max_full"), new("max_taken")
        self.sc_full, self.pt_ready = new("sc_full"), new("pt_ready")
        self.gx_ready = new("gx_ready")
        self.ga_step = new("ga_step")
        self.gT_full, self.gT_free = new("gT_full"), new("gT_free")
        self.gl_full, self.gl_free = new("gl_full"), new("gl_free")
        self.kept = new("kept")
        self.choice_ready = new("choice_ready")
        self.diff_ready, self.exp_ready = new("diff_ready"), new("exp_ready")
        self.rank_full = new("rank_full")
        self.rt_step = new("rt_step")
        self.idx_ready = new("idx_ready")
        self.scattered = new("scattered")
        self.xe_landed = [new(f"xe_landed{i}") for i in range(2)]
        self.w1_landed = [new(f"w1_landed{i}") for i in range(2)]
        self.w2_landed = [new(f"w2_landed{i}") for i in range(2)]
        self.eT_full, self.eT_free = new("eT_full"), new("eT_free")
        self.h_full, self.act_done = new("h_full"), new("act_done")
        self.y_full, self.y_ready = new("y_full"), new("y_ready")
        self.y_stored = [new(f"y_stored{i}") for i in range(2)]
        self.gathered = [new(f"gathered{i}") for i in range(NT // TB)]
        self.combined = new("combined")


class Buffers:
    pass


STAGES = ("moe0", "attn0", "moe0", "attn1f", "moe1", "attn1", "attn1f", "moe1")


def program(nc, a, out):
    ctx = ExitStack()
    with ctx:
        def sb(name, shape, dt=F32):
            return ctx.enter_context(nc.sbuf_tensor(name, [P] + shape, dt))

        k = Buffers()
        k.sig = Signals(lambda name: Signal(ctx.enter_context(nc.semaphore(name))))
        s_in = ctx.enter_context(nc.semaphore("inputs_landed"))
        s_zero = ctx.enter_context(nc.semaphore("zeroed"))
        s_xn = ctx.enter_context(nc.semaphore("xn_zeroed"))
        s_down = ctx.enter_context(nc.semaphore("down_made"))
        s_fill = ctx.enter_context(nc.semaphore("const_filled"))
        s_cast = ctx.enter_context(nc.semaphore("const_cast"))
        s_out = ctx.enter_context(nc.semaphore("stored"))

        x, hid = sb("x", [T * C // P]), sb("hid", [T * C // P])
        k.xn = sb("xn", [T * C // P])
        k.PS = ctx.enter_context(nc.psum_tensor("PS", [P, 8, 512], F32))
        k.ident, k.identb = sb("ident", [P]), sb("identb", [P], BF16)
        k.mask_q, k.mask_k = sb("mask_q", [P], BF16), sb("mask_k", [P], BF16)
        k.tri, k.onesb, k.ones_t = sb("tri", [P], BF16), sb("onesb", [P], BF16), sb("ones_t", [NT])
        down_i = sb("down_i", [16], I32)
        down8, down16 = sb("down8", [8]), sb("down16", [16])
        k.xa, k.st, k.eps = sb("xa", [TB, C]), sb("st", [NT * 6]), sb("eps", [1])
        k.mean, k.dev, k.std, k.rstd, k.rstd2 = (sb(n, [NT]) for n in ("mean", "dev", "std", "rstd", "rstd2"))
        k.xnT = sb("xnT", [S + 2])
        k.xdT = sb("xdT", [S // 2])[:, :]
        k.cv = sb("cv", [2, S // 2])
        k.q32, k.k32 = sb("q32", [S])[:, :], sb("k32", [S])
        k.rest = sb("rest", [S])
        k.parts = sb("parts", [2, 3, S], BF16)
        k.vst = sb("vst", [TB, C])
        k.vs = sb("vs", [G, TB, HG, 32])
        k.qa, k.ka = sb("qa", [G, HG, S], BF16), sb("ka", [G, HG, S], BF16)
        k.mx = sb("mx", [2, 16])
        k.nm32 = sb("nm32", [2, P])[0:16]
        k.nm = sb("nm", [2, 3, P], BF16)[0:16]
        k.osb = sb("osb", [S])[:, :]
        k.rec = sb("rec", [TB, HG])
        k.ctx, k.tmp = sb("ctx", [TB, C]), sb("tmp", [TB, C])
        k.ctxT = sb("ctxT", [S])[:, :]
        k.pt = sb("pt", [2, 5120])
        k.rows_back = k.pt[:, :, 0:NT * C].rearrange("p c (t d) -> p c t d", d=C)
        k.logits, k.ra, k.rb, k.rc, k.rd = (sb(f"r{i}", [NT * 16]) for i in range(5))
        k.onehot = sb("onehot", [2, NT * 16], BF16)
        k.rv, k.before, k.idx = sb("rv", [10, NT]), sb("before", [16]), sb("idx", [4, NT], I32)
        part = lambda i, n=1: k.pt[:, :, i * S:(i + n) * S]
        k.hT = part(0, FC).rearrange("p e (f n) -> p e f n", f=FC)
        k.w2 = part(4).rearrange("p e (f c) -> p e f c", f=FC)
        k.xe, k.ys = (part(i).rearrange("p e (t c) -> p e t c", c=C) for i in (5, 6))
        k.xeT, k.w1 = part(7), part(8)
        k.q_dram = nc.dram_tensor("q_parts", (NPROD, D, H, S), BF16).ap()
        k.k_dram = nc.dram_tensor("k_parts", (NPROD, D, H, S), BF16).ap()
        SLOTS = 2 * T
        k.x_slots = nc.dram_tensor("x_slots", (SLOTS, C), F32).ap()
        k.y_slots = nc.dram_tensor("y_slots", (SLOTS, C), F32).ap()

        loads = [(x[:, :].rearrange("p (t c) -> p t c", c=C), a["x"].rearrange("b (t p) c -> p (b t) c", p=P))]

        def weight(name, src, n=C):
            tile = sb(name, [n])
            loads.append((tile[:, :], src))
            return tile[:, :]

        def rows_of(v):
            return v.partition_broadcast(P)

        def column(v):
            return v.rearrange("(p o) -> p o", o=1)

        def attention_weights(tag, q, kk, v, o, qb, kb, vb, ob, ln_w=None, ln_b=None, conv_w=None, conv_b=None):
            m = Buffers()
            m.wq, m.wk = weight(tag + "wq", q), weight(tag + "wk", kk)
            m.wv, m.wo = weight(tag + "wv", v), weight(tag + "wo", o)
            m.qb, m.kb = weight(tag + "qb", column(qb), 1), weight(tag + "kb", column(kb), 1)
            m.vb, m.ob = weight(tag + "vb", rows_of(vb)), weight(tag + "ob", rows_of(ob))
            m.ln_w = m.ln_b = m.conv_w = m.conv_b = None
            if ln_w is not None:
                m.ln_w, m.ln_b = weight(tag + "lw", column(ln_w), 1), weight(tag + "lb", column(ln_b), 1)
            if conv_w is not None:
                m.conv_w, m.conv_b = weight(tag + "cw", conv_w, 3), weight(tag + "cb", column(conv_b), 1)
            return m

        attn0 = attention_weights("a0", a["a0_qw"], a["a0_kw"], a["a0_vw"], a["a0_ow"], a["a0_qb"], a["a0_kb"],
                                  a["a0_vb"], a["a0_ob"], conv_w=a["a0_cw"], conv_b=a["a0_cb"])
        w3, b3 = a["a1_w"], a["a1_b"]
        attn1 = attention_weights("a1", w3[:, 0:C], w3[:, C:2 * C], w3[:, 2 * C:3 * C], a["a1_ow"], b3[0:C],
                                  b3[C:2 * C], b3[2 * C:3 * C], a["a1_ob"])
        attn1f = attention_weights("af", a["f1_qw"], a["f1_kw"], a["f1_vw"], a["f1_ow"], a["f1_qb"], a["f1_kb"],
                                   a["f1_vb"], a["f1_ob"], ln_w=a["f1_l1w"], ln_b=a["f1_l1b"])
        def expert_weights(tag, g, w1, b1, w2, b2, E, down):
            m = Buffers()
            m.wg = weight(tag + "g", g, E)
            m.w1, m.w2 = w1.rearrange("e c f -> (e c) f"), w2.rearrange("e f c -> (e f) c")
            m.b1 = weight(tag + "b1", b1, E * FC)
            m.b2 = weight(tag + "b2", rows_of(b2.rearrange("e c -> (e c)")), E * C)
            m.ln_w = m.ln_b = None
            m.down = down
            return m

        ffn0 = expert_weights("f0", a["f0_g"], a["f0_w1"], a["f0_b1"], a["f0_w2"], a["f0_b2"], 8, down8[:, :])
        ffn0.gelu_tanh, ffn0.counted = True, 256
        ffn1 = expert_weights("f1", a["f1_g"], a["f1_w1"], a["f1_b1"], a["f1_w2"], a["f1_b2"], 16, down16[:, :])
        ffn1.gelu_tanh, ffn1.counted = False, T
        ffn1.ln_w, ffn1.ln_b = weight("l2w", rows_of(a["f1_l2w"])), weight("l2b", rows_of(a["f1_l2b"]))

        with nc.Block() as block:
            @block.sync
            def _(sp):
                for tile, source in loads:
                    sp.dma_start(tile, source).then_inc(s_in, 16)
                sp.wait_ge(s_xn, 1)
                for half in range(2):
                    n = SLOTS // 2
                    sp.dma_start(k.x_slots[half * n:(half + 1) * n, :].rearrange("(p r) c -> p (r c)", p=P),
                                 k.xn[:, :]).then_inc(s_zero, 16)
                sp.wait_ge(s_in, 16 * len(loads))
                sp.wait_ge(s_zero, 32)

            @block.vector
            def _(dve):
                nc.vector.memset(k.xn[:, :], 0.0).then_inc(s_xn, 1)
                nc.vector.memset(k.qa[:, :, :, :], 0.0)
                nc.vector.memset(k.ka[:, :, :, :], 0.0).then_inc(s_cast, 1)
                nc.vector.memset(k.vs[:, :, :, :, :], 0.0).then_inc(s_cast, 1)
                nc.vector.memset(k.onesb[:, :], 1.0)
                nc.vector.memset(k.ones_t[:, :], 1.0)
                nc.vector.memset(k.eps[:, :], EPS)
                nc.vector.memset(k.xnT[:, 0:1], 0.0)
                dve.wait_ge(s_cast, 2)
                nc.vector.memset(k.ka[64:96, :, :, :], 1.0)
                nc.vector.memset(k.vs[:, :, :, :, D:D + 1], 1.0)
                dve.wait_ge(s_down, 1)
                nc.vector.tensor_copy(down16[:, :], down_i[:, :])
                nc.vector.tensor_scalar(down8[:, :], down_i[:, 0:8], -8.0, None, ALU.add)

            @block.gpsimd
            def _(pool):
                pool.iota(down_i[:, :], pattern=[[-1, 16]], base=16, channel_multiplier=0).then_inc(s_down, 1)
                pool.memset(k.ident[:, :], 0.0)
                pool.memset(k.identb[:, :], 0.0)
                pool.memset(k.mask_q[:, :], 0.0)
                pool.memset(k.mask_k[:, :], 0.0)
                pool.memset(k.tri[:, :], 1.0).then_inc(s_fill, 1)
                pool.wait_ge(s_fill, 1)
                for m in (k.ident, k.identb):
                    pool.affine_select(out=m[:, :], in_=m[:, :], compare_op=ALU.not_equal, fill=1.0, base=0,
                                       pattern=[[-1, P]], channel_multiplier=1)
                pool.affine_select(out=k.mask_q[:, :], in_=k.mask_q[:, :], compare_op=ALU.is_ge, fill=MASKED, base=0,
                                   pattern=[[-1, P]], channel_multiplier=1)
                pool.affine_select(out=k.mask_k[:, :], in_=k.mask_k[:, :], compare_op=ALU.is_ge, fill=MASKED, base=0,
                                   pattern=[[1, P]], channel_multiplier=-1)
                pool.affine_select(out=k.tri[:, :], in_=k.tri[:, :], compare_op=ALU.is_gt, fill=0.0, base=0,
                                   pattern=[[1, P]], channel_multiplier=-1)

        for stage in STAGES:
            if stage == "moe0":
                moe(nc, k, ffn0, x, x, 8, 256, 0.5, ("add", 1e-9), 0.0)
            elif stage == "attn0":
                attention(nc, k, attn0, x, x, False)
            elif stage == "attn1f":
                attention(nc, k, attn1f, x, hid, True, twice=True)
            elif stage == "moe1":
                moe(nc, k, ffn1, hid, x, 16, 2 * T // 16, 0.5 * 0.8, ("max", 1.1920929e-07), 0.5)
            elif stage == "attn1":
                attention(nc, k, attn1, x, x, True)

        with nc.Block() as block:
            @block.sync
            def _(sp):
                sp.dma_start(out.rearrange("b (t p) c -> p (b t) c", p=P),
                             x[:, :].rearrange("p (t c) -> p t c", c=C)).then_inc(s_out, 16)
                sp.wait_ge(s_out, 16)


def layout(np, i):
    t = lambda n: np.ascontiguousarray(i[n].T)
    b1 = lambda n: np.ascontiguousarray(i[n].reshape(-1, FC, P).transpose(2, 0, 1).reshape(P, -1))
    return {
        "x": i["L0_attn_x"],
        "a0_qw": t("L0_attn_q_w"), "a0_kw": t("L0_attn_k_w"), "a0_vw": t("L0_attn_v_w"), "a0_ow": t("L0_attn_out_w"),
        "a0_qb": i["L0_attn_q_b"], "a0_kb": i["L0_attn_k_b"], "a0_vb": i["L0_attn_v_b"], "a0_ob": i["L0_attn_out_b"],
        "a0_cw": i["L0_attn_conv_w"].reshape(C, 3), "a0_cb": i["L0_attn_conv_b"],
        "f0_g": i["L0_ffn_Wg"], "f0_w1": i["L0_ffn_W1"], "f0_b1": b1("L0_ffn_b1"), "f0_w2": i["L0_ffn_W2"],
        "f0_b2": i["L0_ffn_b2"],
        "a1_w": t("L1_attn_qkv_w"), "a1_b": i["L1_attn_qkv_b"], "a1_ow": t("L1_attn_out_w"), "a1_ob": i["L1_attn_out_b"],
        "f1_l1w": i["L1_ffn_ln1_w"], "f1_l1b": i["L1_ffn_ln1_b"],
        "f1_qw": i["L1_ffn_q_w"], "f1_kw": i["L1_ffn_k_w"], "f1_vw": i["L1_ffn_v_w"], "f1_ow": i["L1_ffn_o_w"],
        "f1_qb": i["L1_ffn_q_b"], "f1_kb": i["L1_ffn_k_b"], "f1_vb": i["L1_ffn_v_b"], "f1_ob": i["L1_ffn_o_b"],
        "f1_l2w": i["L1_ffn_ln2_w"], "f1_l2b": i["L1_ffn_ln2_b"], "f1_g": i["L1_ffn_router_w"],
        "f1_w1": i["L1_ffn_fc1_w"], "f1_b1": b1("L1_ffn_fc1_b"), "f1_w2": i["L1_ffn_fc2_w"], "f1_b2": i["L1_ffn_fc2_b"],
    }


def kernel(**inputs):
    import numpy as np
    import concourse.bacc as bacc
    from concourse.bass_utils import run_bass_kernel_spmd

    nc = bacc.Bacc("TRN2", target_bir_lowering=False, num_devices=1)
    arrays, args = {}, {}
    for name, array in layout(np, {n: np.asarray(v) for n, v in inputs.items()}).items():
        array = np.ascontiguousarray(array)
        arrays[f"in_{name}"] = array
        args[name] = nc.dram_tensor(f"in_{name}", array.shape, mybir.dt.from_np(array.dtype), kind="ExternalInput").ap()
    out = nc.dram_tensor("out", (B, S, C), F32, kind="ExternalOutput").ap()
    program(nc, args, out)
    r = run_bass_kernel_spmd(nc, [arrays], core_ids=[0])
    return r.results[0]["out"]
```

```python
from contextlib import ExitStack

import concourse.bass as bass
from concourse import mybir

P = 128
F32 = mybir.dt.float32
BF16 = mybir.dt.bfloat16
I32 = mybir.dt.int32
ALU = mybir.AluOpType
ACT = mybir.ActivationFunctionType
AX = mybir.AxisListType

B, S, C = 8, 512, 128
T = B * S
NT = T // P
TB = S // P
H, D = 16, 8
G = 4
HG = H // G
SCORE_SCALE = float(D) ** -0.5
EPS = 1e-5
MASKED = -1e30
FH = 512
FC = FH // P

Q_PARTS = (0, 0, 1, 0, 2, 1)
K_PARTS = (0, 1, 0, 2, 0, 1)
NPROD = len(Q_PARTS)
ROWS = NPROD * D
MROW = 66
KMAX = MROW
KSC = MROW + 3

SC_BANK = 0
MX_BANK = 4
O_BANK = 6
MISC = 7
GT_BANKS, GL_BANK = (0, 6), 1
XT_BANK, H_BANK, Y_BANK = 0, 2, 6
INV_BANK = Y_BANK


class Signal:

    def __init__(self, handle):
        self.h, self.base = handle, 0

    def at(self, n):
        return self.h, n + self.base


def broadcast_rows(ap, n):
    return ap.unsqueeze(1).to_broadcast([P, n, ap.shape[1]])


def broadcast_last(ap, n):
    return ap.unsqueeze(2).to_broadcast([P, ap.shape[1], n])


def statistics(nc, k, dve, src, twice):
    s, half = k.sig, C // 2

    def tiles(b):
        for t in range(TB):
            ins = nc.vector.bn_stats(k.st[:, bass.ds(b * (TB * 6) + t * 6, 6)], src[:, bass.ds(b * S + t * P, P)])
        ins.then_inc(s.ln_stats.h, 1)

    tiles(0)
    with dve.Fori(1, B, 1) as b:
        tiles(b)
    dve.wait_ge(*s.ln_stats.at(B))
    st = k.st[:, :].rearrange("p (t n) -> p t n", n=6)
    mean, dev, both = k.mean[:, :], k.dev[:, :], k.rstd[:, :]
    nc.vector.tensor_tensor(mean, st[:, :, 1], st[:, :, 4], ALU.add)
    nc.vector.tensor_tensor(dev, st[:, :, 1], st[:, :, 4], ALU.subtract)
    nc.vector.tensor_tensor(both, st[:, :, 2], st[:, :, 5], ALU.add).then_inc(s.ln_step.h, 1)
    dve.wait_ge(*s.ln_step.at(1))
    nc.vector.tensor_scalar(mean, mean, 0.5, None, ALU.mult)
    nc.vector.tensor_tensor(dev, dev, dev, ALU.mult).then_inc(s.ln_step.h, 1)
    dve.wait_ge(*s.ln_step.at(2))
    nc.vector.scalar_tensor_tensor(dev, dev, half / 2.0, both, ALU.mult, ALU.add).then_inc(s.ln_var.h, 1)
    dve.wait_ge(*s.ln_std.at(1))
    nc.vector.reciprocal(k.rstd[:, :], k.std[:, :]).then_inc(s.ln_rstd.h, 1)
    dve.wait_ge(*s.ln_rstd.at(1))
    if twice:
        nc.vector.tensor_tensor(dev, dev, k.rstd[:, :], ALU.mult).then_inc(s.ln_step.h, 1)
        dve.wait_ge(*s.ln_step.at(3))
        nc.vector.tensor_tensor(dev, dev, k.rstd[:, :], ALU.mult).then_inc(s.ln_var.h, 1)
        dve.wait_ge(*s.ln_std.at(2))
        nc.vector.reciprocal(k.rstd2[:, :], k.std[:, :]).then_inc(s.ln_step.h, 1)
        dve.wait_ge(*s.ln_step.at(4))
        nc.vector.tensor_tensor(k.rstd2[:, :], k.rstd2[:, :], k.rstd[:, :], ALU.mult).then_inc(s.ln_rstd.h, 1)
        dve.wait_ge(*s.ln_rstd.at(2))


def deviations(nc, k, act, twice):
    s = k.sig
    for n in range(1 + twice):
        act.wait_ge(*s.ln_var.at(n + 1))
        nc.scalar.activation(k.std[:, :], k.dev[:, :], ACT.Sqrt, bias=k.eps[:, 0:1], scale=1.0 / C).then_inc(s.ln_std.h, 1)


def normalise(nc, k, src, b, scale, dst):
    for t in range(TB):
        ins = nc.vector.tensor_scalar(dst(t), src[:, bass.ds(b * S + t * P, P)], k.mean[:, bass.ds(b * TB + t, 1)],
                                      scale[:, bass.ds(b * TB + t, 1)], ALU.subtract, ALU.mult)
    return ins


def attention(nc, k, w, src, dst, causal, twice=False):
    s, PS = k.sig, k.PS
    conv = w.conv_w is not None
    nk = S // 2 if conv else S
    KB = nk // P
    if causal:
        chunks = [(0, (0, 1), 512), (0, (2, 3), 512), (1, (0, 1), 384), (1, (2, 3), 384),
                  (2, (0, 1, 2, 3), 256), (3, (0, 1, 2, 3), 128)]
        maxes = ([(0, (0, 1, 2, 3), 128)] + [(1, (2 * i, 2 * i + 1), 256) for i in range(2)]
                 + [(2, (i,), 384) for i in range(4)] + [(3, (i,), 512) for i in range(4)])
    else:
        chunks = [(kb, (2 * i, 2 * i + 1), 512) for kb in range(KB) for i in range(2)]
        maxes = [(qb, (2 * i, 2 * i + 1), nk) for qb in range(TB) for i in range(2)]
    NCH, NMX = len(chunks), len(maxes)
    at = [sum(len(c[1]) * c[2] for c in chunks[:i]) for i in range(NCH)]

    def sc_bank(c, i):
        _, heads, n = chunks[c]
        per = 512 // n if len(heads) > 2 else 1
        return SC_BANK + 2 * (c % 2) + i // per, (i % per) * n

    def order(first, last, g):
        has_prev = not (first and g == 0)
        has_max = not (last and g >= 2)
        proj = g == 0 and not last
        plan = []
        mx = [("max", i) for i in range(NMX)] if has_max else []
        take = -(-NMX // NCH)
        for c in range(NCH):
            plan.append(("score", c))
            if c == 0 and has_prev:
                plan.append(("value_p", KB - 1))
            if c == 1 and has_prev:
                plan.append(("o_out", 0))
            plan += mx[:take]
            mx = mx[take:]
            if c == 1 and proj:
                plan += [("norm", 0), ("x_T", 0)]
            if c == 2 and has_prev:
                plan.append(("o_T", 0))
            for kb in range(KB - 1):
                if c == max(i for i in range(NCH) if chunks[i][0] == kb) + 1:
                    plan.append(("value", kb))
            if c == 2 and proj:
                plan.append(("q", 0))
            if c == 3:
                if has_prev and g == 0:
                    plan.append(("ctx_T", 0))
                if proj:
                    plan.append(("k", 0))
                if has_prev and g == 0:
                    plan.append(("out", 0))
                if proj:
                    plan.append(("v", 0))
        plan += mx
        if has_max:
            plan.append(("max_T", 0))
        return plan

    def ahead(b, g):
        return (b, g + 2, 4 * b + g + 2) if g < 2 else (b + 1, g - 2, 4 * b + g + 2)

    with nc.Block() as block:

        @block.tensor
        def _(pe):
            misc = [None]

            def take_misc():
                if misc[0] is not None:
                    pe.wait_ge(*misc[0][0].at(misc[0][1]))

            def max_tile(bb, gg, u, t):
                qb, heads, n = maxes[t]
                if t == 0:
                    pe.wait_ge(*s.qk_landed[gg].at(32 * (bb + 1)))
                if not (isinstance(u, int) and u * NMX + t < 2):
                    pe.wait_ge(*s.max_taken.at(u * NMX + t - 1))
                bank = MX_BANK + (gg * NMX + t) % 2
                for i, h in enumerate(heads):
                    mm = pe.matmul(PS[:, bank, i * n:(i + 1) * n], k.qa[0:KMAX, gg, h, qb * P:(qb + 1) * P],
                                   k.ka[0:KMAX, gg, h, 0:n], start=True, stop=not causal)
                    if causal:
                        mm = pe.matmul(PS[:, bank, (i + 1) * n - P:(i + 1) * n], k.identb[:, :],
                                       k.mask_q[:, :], start=False, stop=True)
                mm.then_inc(s.max_full.h, 1)

            def max_transpose(bb, gg, u):
                pe.wait_ge(*s.max_taken.at((u + 1) * NMX))
                take_misc()
                pe.transpose(PS[0:16, MISC, 0:P], k.mx[:, gg % 2, :], k.ident[:, :]).then_inc(s.mT_full.h, 1)
                misc[0] = (s.mT_free, u + 1)

            def project(name, b1):
                if name == "x_T":
                    pe.wait_ge(*s.xa_ready.at(b1 + 1))
                    take_misc()
                    for t in range(TB):
                        mm = pe.transpose(PS[:, MISC, t * P:(t + 1) * P], k.xa[:, t, :], k.ident[:, :])
                    mm.then_inc(s.xT_full.h, 1)
                    misc[0] = (s.xT_free, b1 + 1)
                if name == "q":
                    take_misc()
                    pe.matmul(PS[:, MISC, :], w.wq, k.xnT[:, 1:S + 1], start=True, stop=True).then_inc(s.q_full.h, 1)
                    misc[0] = (s.q_free, b1 + 1)
                kv = k.xdT if conv else k.xnT[:, 1:S + 1]
                if name == "k":
                    if conv:
                        pe.wait_ge(*s.xd_ready.at(b1 + 1))
                    take_misc()
                    pe.matmul(PS[:, MISC, 0:nk], w.wk, kv[:, 0:nk], start=True, stop=True).then_inc(s.k_full.h, 1)
                    misc[0] = (s.k_free, b1 + 1)
                if name == "v":
                    take_misc()
                    for t in range(KB):
                        mm = pe.matmul(PS[:, MISC, t * P:(t + 1) * P], kv[:, t * P:(t + 1) * P], w.wv,
                                       start=True, stop=True)
                    mm.then_inc(s.v_full.h, 1)
                    misc[0] = (s.v_free, b1 + 1)

            def values(b, g, u, kb):
                if kb == 0:
                    pe.wait_ge(*s.vs_ready.at(u + 1))
                    if not (isinstance(u, int) and u < 1):
                        pe.wait_ge(*s.o_free.at(u))
                last = max(i for i in range(NCH) if chunks[i][0] == kb)
                pe.wait_ge(*s.pt_ready.at(u * NCH + last + 1))
                q0 = kb * P if causal else 0
                for c, (kk, heads, n) in enumerate(chunks):
                    if kk != kb:
                        continue
                    for i, h in enumerate(heads):
                        mm = pe.matmul(PS[32 * h:32 * h + 32, O_BANK, q0:S], k.vs[:, g, kb, h, :],
                                       k.pt[:, g % 2, at[c] + i * n:at[c] + (i + 1) * n],
                                       start=(kb == 0), stop=(kb == KB - 1))
                if kb == KB - 1:
                    mm.then_inc(s.pv_done.h, 1)

            def tail(name, b, g, u):
                if name == "o_T":
                    pe.wait_ge(*s.o_free.at(u + 1))
                    take_misc()
                    for q in range(TB):
                        mm = pe.transpose(PS[:, MISC, q * P:(q + 1) * P], k.osb[:, q * P:(q + 1) * P], k.ident[:, :])
                    mm.then_inc(s.oT_full.h, 1)
                    misc[0] = (s.oT_free, u + 1)
                if name == "ctx_T":
                    take_misc()
                    for q in range(TB):
                        mm = pe.transpose(PS[:, MISC, q * P:(q + 1) * P], k.ctx[:, q, :], k.ident[:, :])
                    mm.then_inc(s.cT_full.h, 1)
                    misc[0] = (s.cT_free, b + 1)
                if name == "out":
                    take_misc()
                    for q in range(TB):
                        mm = pe.matmul(PS[:, MISC, q * P:(q + 1) * P], k.ctxT[:, q * P:(q + 1) * P], w.wo,
                                       start=True, stop=True)
                    mm.then_inc(s.out_full.h, 1)
                    misc[0] = (s.out_free, b + 1)

            def score_chunk(b, g, u, c):
                kb, heads, n = chunks[c]
                if c == 0:
                    pe.wait_ge(*s.m_landed[g].at(48 * (b + 1)))
                if not (isinstance(u, int) and u * NCH + c < 2):
                    pe.wait_ge(*s.pt_ready.at(u * NCH + c - 1))
                q0 = kb * P if causal else 0
                for i, h in enumerate(heads):
                    bank, col = sc_bank(c, i)
                    mm = pe.matmul(PS[:, bank, col:col + n], k.ka[0:KSC, g, h, kb * P:(kb + 1) * P],
                                   k.qa[0:KSC, g, h, q0:S], start=True, stop=not causal)
                    if causal:
                        mm = pe.matmul(PS[:, bank, col:col + P], k.identb[:, :], k.mask_k[:, :],
                                       start=False, stop=True)
                mm.then_inc(s.sc_full.h, 1)

            def batch(b, first, last):
                misc[0] = (s.mT_free, 4 * b + 2)
                for g in range(G):
                    u = 4 * b + g
                    pb, pg = (b, g - 1) if g else (b - 1, G - 1)
                    for name, i in order(first, last, g):
                        if name == "score":
                            score_chunk(b, g, u, i)
                        elif name == "value":
                            values(b, g, u, i)
                        elif name == "value_p":
                            values(pb, pg, u - 1, i)
                        elif name == "max":
                            max_tile(*ahead(b, g), i)
                        elif name == "max_T":
                            max_transpose(*ahead(b, g))
                        elif name in ("x_T", "q", "k", "v"):
                            project(name, b + 1)
                        elif name in ("o_T", "ctx_T", "out"):
                            tail(name, pb, pg, u - 1)

            for name in ("x_T", "q", "k", "v"):
                project(name, 0)
            for g in range(2):
                for t in range(NMX):
                    max_tile(0, g, g, t)
                max_transpose(0, g, g)
            batch(0, True, False)
            with pe.Fori(1, B - 1, 1) as b:
                batch(b, False, False)
            batch(B - 1, False, True)
            values(B - 1, G - 1, 4 * B - 1, KB - 1)
            for name in ("o_T", "ctx_T", "out"):
                tail(name, B - 1, G - 1, 4 * B - 1)

        @block.scalar
        def _(act):
            def chunk(g, u, c):
                kb, heads, n = chunks[c]
                act.wait_ge(*s.sc_full.at(u * NCH + c + 1))
                if c == 0 and not (isinstance(u, int) and u < 2):
                    act.wait_ge(*s.pv_done.at(u - 1))
                b0 = SC_BANK + 2 * (c % 2)
                nb = 1 if len(heads) * n <= 512 else 2
                per = len(heads) // nb
                scores = PS[:, b0:b0 + nb, 0:per * n]
                probs = k.pt[:, g % 2, at[c]:at[c] + len(heads) * n].rearrange("p (b n) -> p b n", b=nb)
                nc.scalar.activation(probs, scores, ACT.Exp, scale=SCORE_SCALE).then_inc(s.pt_ready.h, 1)

            def copy(name, b, u):
                if name == "x_T":
                    act.wait_ge(*s.xT_full.at(b + 1))
                    if not (isinstance(b, int) and b < 1):
                        act.wait_ge(*s.v_full.at(b))
                        if conv:
                            act.wait_ge(*s.xd_ready.at(b))
                    if w.ln_w is not None:
                        nc.scalar.activation(k.xnT[:, 1:S + 1], PS[:, MISC, :], ACT.Identity, scale=w.ln_w,
                                             bias=w.ln_b).then_inc(s.xT_free.h, 1)
                    else:
                        nc.scalar.activation(k.xnT[:, 1:S + 1], PS[:, MISC, :], ACT.Copy).then_inc(s.xT_free.h, 1)
                if name == "q":
                    act.wait_ge(*s.q_full.at(b + 1))
                    if not (isinstance(b, int) and b < 1):
                        act.wait_ge(*s.pq_ready.at(2 * b))
                    nc.scalar.activation(k.q32, PS[:, MISC, :], ACT.Identity, bias=w.qb).then_inc(s.q_free.h, 1)
                if name == "k":
                    act.wait_ge(*s.k_full.at(b + 1))
                    nc.scalar.activation(k.k32[:, 0:nk], PS[:, MISC, 0:nk], ACT.Identity, bias=w.kb).then_inc(s.k_free.h, 1)
                if name == "o_out":
                    act.wait_ge(*s.pv_done.at(u + 1))
                    if not (isinstance(u, int) and u < 1):
                        act.wait_ge(*s.oT_full.at(u))
                    nc.scalar.activation(k.osb, PS[:, O_BANK, :], ACT.Copy).then_inc(s.o_free.h, 1)
                if name == "ctx_T":
                    act.wait_ge(*s.cT_full.at(b + 1))
                    nc.scalar.activation(k.ctxT, PS[:, MISC, :], ACT.Copy).then_inc(s.cT_free.h, 1)

            def batch(b, first, last):
                for g in range(G):
                    u = 4 * b + g
                    pb = b if g else b - 1
                    for name, i in order(first, last, g):
                        if name == "score":
                            chunk(g, u, i)
                        elif name in ("x_T", "q", "k"):
                            copy(name, b + 1, u)
                        elif name in ("o_out", "ctx_T"):
                            copy(name, pb, u - 1)

            deviations(nc, k, act, twice)
            for name in ("x_T", "q", "k"):
                copy(name, 0, 0)
            batch(0, True, False)
            with act.Fori(1, B - 1, 1) as b:
                batch(b, False, False)
            batch(B - 1, False, True)
            for name in ("o_out", "ctx_T"):
                copy(name, B - 1, 4 * B - 1)

        @block.vector
        def _(dve):
            def norm(b):
                if not (isinstance(b, int) and b < 1):
                    dve.wait_ge(*s.xT_full.at(b))
                if twice:
                    normalise(nc, k, src, b, k.rstd, lambda t: dst[:, bass.ds(b * S + t * P, P)])
                normalise(nc, k, src, b, k.rstd2 if twice else k.rstd, lambda t: k.xa[:, t, :]).then_inc(s.xa_ready.h, 1)

            def project(name, b1):
                if name == "x_T":
                    if conv:
                        dve.wait_ge(*s.xT_free.at(b1 + 1))
                        if not (isinstance(b1, int) and b1 < 1):
                            dve.wait_ge(*s.xd_ready.at(b1))
                        tap = lambda j: k.xnT[:, j:j + S].rearrange("p (t two) -> p t two", two=2)[:, :, 0]
                        nc.vector.tensor_scalar(k.cv[:, 0, :], tap(1), w.conv_w[:, 1:2], w.conv_b,
                                                ALU.mult, ALU.add).then_inc(s.cv_step.h, 1)
                        dve.wait_ge(*s.cv_step.at(2 * b1 + 1))
                        nc.vector.scalar_tensor_tensor(k.cv[:, 1, :], tap(0), w.conv_w[:, 0:1], k.cv[:, 0, :],
                                                       ALU.mult, ALU.add).then_inc(s.cv_step.h, 1)
                        dve.wait_ge(*s.cv_step.at(2 * b1 + 2))
                        nc.vector.scalar_tensor_tensor(k.xdT, tap(2), w.conv_w[:, 2:3], k.cv[:, 1, :],
                                                       ALU.mult, ALU.add).then_inc(s.xd_ready.h, 1)
                if name == "v":
                    dve.wait_ge(*s.v_full.at(b1 + 1))
                    if not (isinstance(b1, int) and b1 < 1):
                        dve.wait_ge(*s.vs_ready.at(4 * b1))
                    nc.vector.tensor_tensor(k.vst[:, 0:KB, :], PS[:, MISC, 0:KB * P].rearrange("p (t c) -> p t c", c=P),
                                            broadcast_rows(w.vb, KB), ALU.add).then_inc(s.v_free.h, 1)

            def max_tile(bb, gg, u, t):
                qb, heads, n = maxes[t]
                dve.wait_ge(*s.max_full.at(u * NMX + t + 1))
                if t == 0 and not (isinstance(u, int) and u < 2):
                    dve.wait_ge(*s.mT_full.at(u - 1))
                bank = MX_BANK + (gg * NMX + t) % 2
                out = k.mx[:, gg % 2, :].rearrange("p (h q) -> p h q", q=TB)[:, heads[0]:heads[-1] + 1, qb]
                nc.vector.tensor_reduce(out, PS[:, bank, 0:len(heads) * n].rearrange("p (h n) -> p h n", n=n),
                                        AX.X, ALU.max).then_inc(s.max_taken.h, 1)

            def max_split(gg, u, used=None):
                dve.wait_ge(*s.mT_full.at(u + 1))
                if not (isinstance(u, int) and u < 1):
                    dve.wait_ge(*s.nm_ready.at(u))
                nc.vector.tensor_scalar(k.nm32[:, 0, :], PS[0:16, MISC, 0:P], -1.0, None, ALU.mult).then_inc(s.mT_free.h, 1)
                dve.wait_ge(*s.mT_free.at(u + 1))
                if used is not None:
                    dve.wait_ge(*s.m_landed[used[0]].at(used[1]))
                nc.vector.tensor_copy(k.nm[:, gg % 2, 0, :], k.nm32[:, 0, :]).then_inc(s.nm_step.h, 1)
                dve.wait_ge(*s.nm_step.at(3 * u + 1))
                nc.vector.tensor_tensor(k.nm32[:, 1, :], k.nm32[:, 0, :], k.nm[:, gg % 2, 0, :], ALU.subtract).then_inc(s.nm_step.h, 1)
                dve.wait_ge(*s.nm_step.at(3 * u + 2))
                nc.vector.tensor_copy(k.nm[:, gg % 2, 1, :], k.nm32[:, 1, :]).then_inc(s.nm_step.h, 1)
                dve.wait_ge(*s.nm_step.at(3 * u + 3))
                nc.vector.tensor_tensor(k.nm[:, gg % 2, 2, :], k.nm32[:, 1, :], k.nm[:, gg % 2, 1, :], ALU.subtract).then_inc(s.nm_ready.h, 1)

            def tail(name, b, g, u):
                if name == "o_T":
                    dve.wait_ge(*s.oT_full.at(u + 1))
                    o_T = PS[:, MISC, :].rearrange("p (q h c) -> p q h c", q=TB, h=HG)
                    nc.vector.reciprocal(k.rec[:, :, :], o_T[:, :, :, D]).then_inc(s.rec_done.h, 1)
                    dve.wait_ge(*s.rec_done.at(u + 1))
                    if g == 0 and not (isinstance(b, int) and b < 1):
                        dve.wait_ge(*s.cT_full.at(b))
                    nc.vector.tensor_tensor(k.ctx[:, :, g * 32:g * 32 + 32].rearrange("p q (h d) -> p q h d", h=HG),
                                            o_T[:, :, :, 0:D], k.rec[:, :, :].unsqueeze(3).to_broadcast([P, TB, HG, D]),
                                            ALU.mult).then_inc(s.oT_free.h, 1)
                if name == "out":
                    dve.wait_ge(*s.out_full.at(b + 1))
                    if not (isinstance(b, int) and b < 1):
                        dve.wait_ge(*s.res_done.at(b))
                    nc.vector.tensor_tensor(k.tmp[:, :, :], PS[:, MISC, :].rearrange("p (q c) -> p q c", c=P),
                                            broadcast_rows(w.ob, TB), ALU.add).then_inc(s.out_free.h, 1)
                    dve.wait_ge(*s.out_free.at(b + 1))
                    dve.wait_ge(*s.xa_ready.at(b + 1))
                    residual = dst if twice else src
                    nc.vector.tensor_tensor(dst[:, bass.ds(b * S, S)], residual[:, bass.ds(b * S, S)],
                                            k.tmp[:, :, :].rearrange("p q c -> p (q c)"), ALU.add).then_inc(s.res_done.h, 1)

            def batch(b, first, last):
                for g in range(G):
                    u = 4 * b + g
                    pb, pg = (b, g - 1) if g else (b - 1, G - 1)
                    for name, i in order(first, last, g):
                        if name == "norm":
                            norm(b + 1)
                        elif name in ("x_T", "q", "k", "v"):
                            project(name, b + 1)
                        elif name == "max":
                            max_tile(*ahead(b, g), i)
                        elif name == "max_T":
                            bb, gg, uu = ahead(b, g)
                            max_split(gg, uu, used=(g, 48 * (b + 1)))
                        elif name in ("o_out", "o_T", "ctx_T", "out"):
                            tail(name, pb, pg, u - 1)

            statistics(nc, k, dve, src, twice)
            norm(0)
            for name in ("x_T", "q", "k", "v"):
                project(name, 0)
            for g in range(2):
                for t in range(NMX):
                    max_tile(0, g, g, t)
                max_split(g, g)
            batch(0, True, False)
            with dve.Fori(1, B - 1, 1) as b:
                batch(b, False, False)
            batch(B - 1, False, True)
            for name in ("o_out", "o_T", "ctx_T", "out"):
                tail(name, B - 1, G - 1, 4 * B - 1)

        @block.gpsimd
        def _(pool):
            def split(side, b):
                full, n = (k.q32, S) if side == 0 else (k.k32[:, 0:nk], nk)
                pool.wait_ge(*(s.q_free if side == 0 else s.k_free).at(b + 1))
                if side == 0 and not (isinstance(b, int) and b < 1):
                    pool.wait_ge(*s.parts_written.at(16 * 2 * NPROD * b))
                hi, mid, lo = (k.parts[:, side, j, 0:n] for j in range(3))
                pool.tensor_copy(hi, full).then_inc(s.sp_hi.h, 1)
                pool.wait_ge(*s.sp_hi.at(2 * b + side + 1))
                pool.tensor_tensor(k.rest[:, 0:n], full, hi, ALU.subtract).then_inc(s.sp_rest.h, 1)
                pool.wait_ge(*s.sp_rest.at(2 * b + side + 1))
                pool.tensor_copy(mid, k.rest[:, 0:n]).then_inc(s.sp_mid.h, 1)
                pool.wait_ge(*s.sp_mid.at(2 * b + side + 1))
                pool.tensor_tensor(lo, k.rest[:, 0:n], mid, ALU.subtract).then_inc(s.pq_ready.h, 1)
                pool.wait_ge(*s.pq_ready.at(2 * b + side + 1))

            def spread(b, g):
                if g == 0:
                    pool.wait_ge(*s.v_free.at(b + 1))
                if not (isinstance(b, int) and b < 1):
                    pool.wait_ge(*s.pv_done.at(4 * b - 3 + g))
                pool.tensor_copy(k.vs[:, g, 0:KB, :, 0:D], k.vst[:, 0:KB, g * 32:g * 32 + 32]
                                 .rearrange("p t (h d) -> p t h d", h=HG)).then_inc(s.vs_ready.h, 1)

            def batch(b):
                split(0, b)
                split(1, b)
                for g in range(G):
                    spread(b, g)

            for b in range(B):
                batch(b)

        @block.sync
        def _(sp):
            def write_parts(b):
                if not (isinstance(b, int) and b < 1):
                    for g in range(G):
                        sp.wait_ge(*s.qk_landed[g].at(32 * b))
                for side, parts, n, scratch in ((0, Q_PARTS, S, k.q_dram), (1, K_PARTS, nk, k.k_dram)):
                    sp.wait_ge(*s.pq_ready.at(2 * b + side + 1))
                    for r, part in enumerate(parts):
                        sp.dma_start(scratch[r, :, :, 0:n].rearrange("d h t -> h d t"),
                                     k.parts[:, side, part, 0:n]).then_inc(s.parts_written.h, 16)

            def load(b, g):
                sp.wait_ge(*s.parts_written.at(16 * 2 * NPROD * (b + 1)))
                if not (isinstance(b, int) and b < 1):
                    sp.wait_ge(*s.sc_full.at((4 * b - 3 + g) * NCH))
                for arr, scratch, n in ((k.qa, k.q_dram, S), (k.ka, k.k_dram, nk)):
                    sp.dma_start(arr[0:ROWS, g, :, 0:n], scratch[:, :, g * HG:(g + 1) * HG, 0:n]
                                 .rearrange("r d h t -> (r d) h t")).then_inc(s.qk_landed[g].h, 16)

            def put_max(b, g):
                u = 4 * b + g
                sp.wait_ge(*s.nm_ready.at(u + 1))
                for j in range(3):
                    sp.dma_start(k.qa[MROW + j:MROW + j + 1, g, :, :].rearrange("o h (q t) -> o (h q) t", t=P),
                                 k.nm[:, g % 2, j, :]).then_inc(s.m_landed[g].h, 16)

            def batch(b, last):
                if not last:
                    write_parts(b + 1)
                put_max(b, 2)
                if not last:
                    load(b + 1, 0)
                put_max(b, 3)
                if not last:
                    load(b + 1, 1)
                    put_max(b + 1, 0)
                    load(b + 1, 2)
                    put_max(b + 1, 1)
                    load(b + 1, 3)

            write_parts(0)
            for g in range(G):
                load(0, g)
            put_max(0, 0)
            put_max(0, 1)
            for b in range(B):
                batch(b, b == B - 1)

    U = 4 * B
    counts = {
        s.ln_stats: B, s.ln_step: 2 + 2 * twice, s.ln_var: 1 + twice, s.ln_std: 1 + twice,
        s.ln_rstd: 1 + twice, s.xa_ready: B, s.xT_full: B, s.xT_free: B, s.q_full: B,
        s.q_free: B, s.k_full: B, s.k_free: B, s.v_full: B, s.v_free: B, s.cT_full: B, s.cT_free: B,
        s.out_full: B, s.out_free: B, s.res_done: B, s.max_full: U * NMX, s.max_taken: U * NMX,
        s.mT_full: U, s.mT_free: U, s.nm_step: 3 * U, s.nm_ready: U, s.pv_done: U, s.o_free: U, s.oT_full: U,
        s.oT_free: U, s.rec_done: U, s.vs_ready: U, s.sc_full: U * NCH, s.pt_ready: U * NCH,
        s.sp_hi: 2 * B, s.sp_rest: 2 * B, s.sp_mid: 2 * B, s.pq_ready: 2 * B, s.parts_written: 16 * 2 * NPROD * B,
    }
    if conv:
        counts |= {s.cv_step: 2 * B, s.xd_ready: B}
    counts |= {x: 32 * B for x in s.qk_landed} | {x: 48 * B for x in s.m_landed}
    for signal, n in counts.items():
        signal.base += n


def moe(nc, k, w, src, dst, E, capacity, gate_scale, renorm, src_scale):
    s, PS = k.sig, k.PS
    ST = capacity // P
    NE = NT * E
    PAIRS = E // 2
    TILES = E * ST
    TP = 8
    GELU = ACT.Gelu_apprx_tanh if w.gelu_tanh else ACT.Gelu
    NG = NT // TB

    def over_e(ap):
        return ap.unsqueeze(2).to_broadcast([P, NT, E])

    def all_pairs(eng, pair):
        pair(0, False)
        with eng.Fori(1, PAIRS - 1, 1) as j:
            pair(j, False)
        pair(PAIRS - 1, True)

    with nc.Block() as block:

        @block.tensor
        def _(pe):
            def rows_transposed(i):
                pe.wait_ge(*s.gx_ready.at(i + 1))
                if i >= 2:
                    pe.wait_ge(*s.gT_free.at(i - 1))
                for t in range(TB):
                    at = (i * TB + t) * P
                    mm = pe.transpose(PS[:, GT_BANKS[i % 2], t * P:(t + 1) * P], k.xn[:, at:at + P], k.ident[:, :])
                mm.then_inc(s.gT_full.h, 1)

            def route(i):
                pe.wait_ge(*s.gT_free.at(i + 1))
                if i >= 1:
                    pe.wait_ge(*s.gl_free.at(i))
                for t in range(TB):
                    mm = pe.matmul(PS[:, GL_BANK, t * E:(t + 1) * E], k.xnT[:, 1 + t * P:1 + (t + 1) * P], w.wg,
                                   start=True, stop=True)
                mm.then_inc(s.gl_full.h, 1)

            rows_transposed(0)
            for i in range(NG):
                if i + 1 < NG:
                    rows_transposed(i + 1)
                route(i)
            for c in range(2):
                pe.wait_ge(*s.choice_ready.at(c + 1))
                oh = k.onehot[:, c, 0:NE]
                pe.matmul(PS[:, 2 + 2 * c, 0:NE], k.tri[:, :], oh, start=True, stop=True)
                pe.matmul(PS[:, 3 + 2 * c, 0:NE], k.onesb[:, :], oh, start=True, stop=True).then_inc(s.rank_full.h, 1)
            def occupants(c, i, first=False, last=False):
                for n in range(TP):
                    t = i * TP + n
                    mm = pe.matmul(PS[:, INV_BANK, 0:2 * TILES], k.at_rank[:, c, bass.ds(t * P, P)],
                                   k.in_tile[:, c, bass.ds(t * (2 * TILES), 2 * TILES)],
                                   start=first and n == 0, stop=last and n == TP - 1)
                return mm

            pe.wait_ge(*s.marks_ready.at(1))
            occupants(0, 0, first=True)
            with pe.Fori(1, NT // TP, 1) as i:
                occupants(0, i)
            pe.wait_ge(*s.marks_ready.at(2))
            for i in range(NT // TP):
                mm = occupants(1, i, last=(i == NT // TP - 1))
            mm.then_inc(s.inv_full.h, 1)

            def rows_T(j, par):
                e = 2 * j + par
                pe.wait_ge(*s.xe_landed[par].at(16 * ST * (j + 1)))
                if not (isinstance(j, int) and j < 1):
                    pe.wait_ge(*s.eT_free.at(e - 1))
                for t in range(ST):
                    mm = pe.transpose(PS[:, XT_BANK + par, t * P:(t + 1) * P], k.xe[:, par, t, :], k.ident[:, :])
                mm.then_inc(s.eT_full.h, 1)

            def hidden(j, par):
                e = 2 * j + par
                pe.wait_ge(*s.eT_free.at(e + 1))
                pe.wait_ge(*s.w1_landed[par].at(16 * (j + 1)))
                for f in range(FC):
                    if not (isinstance(j, int) and e < 1):
                        pe.wait_ge(*s.act_done.at(e * FC - FC + f + 1))
                    pe.matmul(PS[:, H_BANK + f, 0:capacity], k.w1[:, par, f * P:(f + 1) * P],
                              k.xeT[:, par, 0:capacity], start=True, stop=True).then_inc(s.h_full.h, 1)

            def output(j, par):
                e = 2 * j + par
                pe.wait_ge(*s.w2_landed[par].at(16 * (j + 1)))
                pe.wait_ge(*s.act_done.at(e * FC + FC))
                if not (isinstance(j, int) and j < 1):
                    pe.wait_ge(*s.y_ready.at(e - 1))
                for t in range(ST):
                    for f in range(FC):
                        mm = pe.matmul(PS[:, Y_BANK + par, t * P:(t + 1) * P], k.hT[:, par, f, t * P:(t + 1) * P],
                                       k.w2[:, par, f, :], start=(f == 0), stop=(f == FC - 1))
                mm.then_inc(s.y_full.h, 1)

            def pair(j, last):
                hidden(j, 0)
                rows_T(j, 1)
                output(j, 0)
                hidden(j, 1)
                if not last:
                    rows_T(j + 1, 0)
                output(j, 1)

            rows_T(0, 0)
            all_pairs(pe, pair)

        @block.scalar
        def _(act):
            def route(i):
                act.wait_ge(*s.gT_full.at(i + 1))
                nc.scalar.activation(k.xnT[:, 1:S + 1], PS[:, GT_BANKS[i % 2], :], ACT.Copy).then_inc(s.gT_free.h, 1)
                act.wait_ge(*s.gl_full.at(i + 1))
                nc.scalar.activation(k.logits[:, i * (TB * E):(i + 1) * (TB * E)], PS[:, GL_BANK, 0:TB * E],
                                     ACT.Copy).then_inc(s.gl_free.h, 1)

            deviations(nc, k, act, False)
            for i in range(NG):
                route(i)
            act.wait_ge(*s.diff_ready.at(1))
            nc.scalar.activation(k.ra[:, 0:NE], k.ra[:, 0:NE], ACT.Exp).then_inc(s.exp_ready.h, 1)
            act.wait_ge(*s.diff_ready.at(2))
            nc.scalar.activation(k.rv[:, 6, :], k.rv[:, 6, :], ACT.Exp).then_inc(s.exp_ready.h, 1)

            def pair(j, last):
                for par in range(2):
                    e = 2 * j + par
                    for f in range(FC):
                        act.wait_ge(*s.h_full.at(e * FC + f + 1))
                        if f == 0 and not (isinstance(j, int) and j < 1):
                            act.wait_ge(*s.y_full.at(e - 1))
                        nc.scalar.activation(k.hT[:, par, f, 0:capacity], PS[:, H_BANK + f, 0:capacity], GELU,
                                             bias=w.b1[:, bass.ds(e * FC + f, 1)]).then_inc(s.act_done.h, 1)

            all_pairs(act, pair)

        @block.vector
        def _(dve):
            affine = w.ln_w is not None

            def norm(i):
                rows = lambda t: k.xn[:, bass.ds(i * S + t * P, P)]
                ins = normalise(nc, k, src, i, k.rstd, rows)
                if affine:
                    four = k.xn[:, bass.ds(i * S, S)].rearrange("p (t c) -> p t c", c=C)
                    ins.then_inc(s.ga_step.h, 1)
                    dve.wait_ge(*s.ga_step.at(2 * i + 1))
                    nc.vector.tensor_tensor(four, four, broadcast_rows(w.ln_w, TB), ALU.mult).then_inc(s.ga_step.h, 1)
                    dve.wait_ge(*s.ga_step.at(2 * i + 2))
                    ins = nc.vector.tensor_tensor(four, four, broadcast_rows(w.ln_b, TB), ALU.add)
                ins.then_inc(s.gx_ready.h, 1)

            statistics(nc, k, dve, src, False)
            dve.wait_ge(k.zeroed, 32)
            norm(0)
            with dve.Fori(1, NG, 1) as i:
                norm(i)

            steps = [0]

            def link(ins):
                ins.then_inc(s.rt_step.h, 1)
                steps[0] += 1
                dve.wait_ge(*s.rt_step.at(steps[0]))

            v = lambda n: k.rv[:, n, :]
            e3 = lambda tile: tile[:, 0:NE].rearrange("p (t e) -> p t e", e=E)
            logits, ra, rb, rc, rd = e3(k.logits), e3(k.ra), e3(k.rb), e3(k.rc), e3(k.rd)
            onehot = [k.onehot[:, c, 0:NE].rearrange("p (t e) -> p t e", e=E) for c in range(2)]
            tt, red = nc.vector.tensor_tensor, nc.vector.tensor_reduce
            TOP, LAST = (0, 1), (2, 3)

            def choose(c, values):
                link(red(v(TOP[c]), values, AX.X, ALU.max))
                link(tt(rb, values, over_e(v(TOP[c])), ALU.is_equal))
                link(tt(rb, rb, broadcast_rows(w.down, NT), ALU.mult))
                link(red(v(LAST[c]), rb, AX.X, ALU.max))
                tt(onehot[c], rb, over_e(v(LAST[c])), ALU.is_equal).then_inc(s.choice_ready.h, 1)
                dve.wait_ge(*s.choice_ready.at(c + 1))

            dve.wait_ge(*s.gl_free.at(NG))
            choose(0, logits)
            tt(ra, logits, over_e(v(TOP[0])), ALU.subtract).then_inc(s.diff_ready.h, 1)
            link(nc.vector.scalar_tensor_tensor(rc, onehot[0], MASKED, logits, ALU.mult, ALU.add))
            choose(1, rc)
            tt(v(6), v(TOP[1]), v(TOP[0]), ALU.subtract).then_inc(s.diff_ready.h, 1)
            dve.wait_ge(*s.exp_ready.at(1))
            link(red(v(4), ra, AX.X, ALU.add))
            link(nc.vector.reciprocal(v(4), v(4)))
            dve.wait_ge(*s.exp_ready.at(2))
            link(tt(v(5), v(6), v(4), ALU.mult))

            dve.wait_ge(*s.xn_stored.at(16 * NG))
            for c in range(2):
                dve.wait_ge(*s.rank_full.at(c + 1))
                within = PS[:, 2 + 2 * c, 0:NE].rearrange("p (t e) -> p t e", e=E)
                total = PS[:, 3 + 2 * c, 0:NE].rearrange("p (t e) -> p t e", e=E)
                upto = (rc, rd)[c]
                for e in range(E):
                    ins = nc.vector.tensor_tensor_scan(upto[:, :, e], k.ones_t[:, :], total[:, :, e], 0.0, ALU.mult, ALU.add)
                link(ins)
                link(tt(rb, upto, total, ALU.subtract))
                link(tt(rb, rb, within, ALU.add))
                if c == 1:
                    link(nc.vector.tensor_scalar(k.before[:, 0:E], rc[:, NT - 1, :], float(w.counted), None, ALU.min))
                    link(tt(rb, rb, broadcast_rows(k.before[:, 0:E], NT), ALU.add))
                link(tt(rb, rb, onehot[c], ALU.mult))
                link(red(v(7), rb, AX.X, ALU.add))
                link(nc.vector.tensor_scalar(v(8 + c), v(7), float(capacity), None, ALU.is_lt))
                link(nc.vector.tensor_scalar(v(6), v(7), float(P), None, ALU.is_ge))
                for n in range(2, ST):
                    link(nc.vector.scalar_tensor_tensor(v(6), v(7), float(n * P), v(6), ALU.is_ge, ALU.add))
                link(nc.vector.scalar_tensor_tensor(v(7), v(6), -float(P), v(7), ALU.mult, ALU.add))
                link(nc.vector.scalar_tensor_tensor(v(6), v(LAST[c]), -float(ST), v(6), ALU.mult, ALU.add))
                link(nc.vector.tensor_scalar(v(6), v(6), float(TILES), None, ALU.add))
                tt(k.at_rank[:, c, :].rearrange("p (t r) -> p t r", r=P), broadcast_rows(k.count[:, :], NT),
                   v(7).unsqueeze(2).to_broadcast([P, NT, P]), ALU.is_equal)
                marks = k.in_tile[:, c, 0:NT * 2 * TILES].rearrange("p (t a n) -> p t a n", a=2, n=TILES)
                low, high = marks[:, :, 0, :], marks[:, :, 1, :]
                link(tt(high, broadcast_rows(k.count[:, 0:TILES], NT), v(6).unsqueeze(2).to_broadcast([P, NT, TILES]),
                        ALU.is_equal))
                link(nc.vector.tensor_scalar(low, high, k.lane[:, 0:1], None, ALU.mult))
                tt(high, high, k.row_high[:, c, :].unsqueeze(2).to_broadcast([P, NT, TILES]), ALU.mult)\
                    .then_inc(s.marks_ready.h, 1)
            dve.wait_ge(*s.inv_full.at(1))
            goes, comes = k.ra[:, 0:TILES], k.rb[:, 0:TILES]
            link(nc.vector.tensor_scalar(goes, PS[:, INV_BANK, 0:TILES], float(2 * T), None, ALU.add))
            link(tt(goes, goes, PS[:, INV_BANK, TILES:2 * TILES], ALU.add))
            nc.vector.tensor_copy(k.idx[:, 1, 0:TILES], goes)
            link(nc.vector.tensor_scalar(comes, goes, float(T), None, ALU.is_ge))
            link(nc.vector.scalar_tensor_tensor(comes, comes, -float(T), goes, ALU.mult, ALU.add))
            link(nc.vector.tensor_scalar(comes, comes, float(T - 1), None, ALU.min))
            nc.vector.tensor_copy(k.idx[:, 0, 0:TILES], comes).then_inc(s.idx_ready.h, 1)

            if renorm[0] == "add":
                link(tt(v(6), v(4), v(5), ALU.add))
                link(nc.vector.tensor_scalar(v(6), v(6), renorm[1], None, ALU.add))
            for c in range(2):
                link(tt(v(4 + c), v(4 + c), v(8 + c), ALU.mult))
            if renorm[0] == "max":
                link(tt(v(6), v(4), v(5), ALU.add))
                link(nc.vector.tensor_scalar(v(6), v(6), renorm[1], None, ALU.max))
            link(nc.vector.reciprocal(v(6), v(6)))
            for c in range(2):
                link(nc.vector.scalar_tensor_tensor(v(4 + c), v(4 + c), gate_scale, v(6), ALU.mult, ALU.mult))
            if src_scale:
                for i in range(NG):
                    ins = nc.vector.scalar_tensor_tensor(dst[:, i * S:(i + 1) * S], src[:, i * S:(i + 1) * S], src_scale,
                                                         dst[:, i * S:(i + 1) * S], ALU.mult, ALU.add)
                link(ins)
            k.route_steps = steps[0]

            def rows(j, par):
                e = 2 * j + par
                dve.wait_ge(*s.eT_full.at(e + 1))
                if not (isinstance(j, int) and j < 1):
                    dve.wait_ge(*s.h_full.at((e - 1) * FC))
                nc.vector.tensor_copy(k.xeT[:, par, 0:capacity], PS[:, XT_BANK + par, 0:capacity]).then_inc(s.eT_free.h, 1)

            def result(j, par):
                e = 2 * j + par
                dve.wait_ge(*s.y_full.at(e + 1))
                if not (isinstance(j, int) and j < 1):
                    dve.wait_ge(*s.y_stored[par].at(16 * ST * j))
                b2 = w.b2[:, bass.ds(e * C, C)].unsqueeze(1).to_broadcast([P, ST, C])
                nc.vector.tensor_tensor(k.ys[:, par, 0:ST, :], PS[:, Y_BANK + par, 0:capacity]
                                        .rearrange("p (t c) -> p t c", c=C), b2, ALU.add).then_inc(s.y_ready.h, 1)

            def pair(j, last):
                rows(j, 1)
                result(j, 0)
                if not last:
                    rows(j + 1, 0)
                result(j, 1)

            rows(0, 0)
            all_pairs(dve, pair)

            for i in range(NG):
                dve.wait_ge(*s.gathered[i].at(16 * 2))
                for c in range(2):
                    for t in range(i * TB, (i + 1) * TB):
                        ins = nc.vector.scalar_tensor_tensor(dst[:, t * P:(t + 1) * P], k.rows_back[:, c, t, :],
                                                             k.rv[:, 4 + c, t:t + 1], dst[:, t * P:(t + 1) * P],
                                                             ALU.mult, ALU.add)
                    ins.then_inc(s.combined.h, 1)
                    dve.wait_ge(*s.combined.at(2 * i + c + 1))

        @block.gpsimd
        def _(pool):
            def fetch(e):
                for t in range(ST):
                    n = e * ST + t
                    pool.indirect_dma_start(k.xe[:, e % 2, t, :], None, k.xn_dram[:, :],
                                            bass.IndirectOffsetOnAxis(k.idx[:, 0, n:n + 1], 0),
                                            bounds_check=T - 1, oob_is_err=False).then_inc(s.xe_landed[e % 2].h, 16)

            def deliver(e):
                pool.wait_ge(*s.y_ready.at(e + 1))
                for t in range(ST):
                    n = e * ST + t
                    pool.indirect_dma_start(k.y_rows[:, :], bass.IndirectOffsetOnAxis(k.idx[:, 1, n:n + 1], 0),
                                            k.ys[:, e % 2, t, :], None, bounds_check=2 * T - 1,
                                            oob_is_err=False).then_inc(s.y_stored[e % 2].h, 16)

            pool.wait_ge(*s.xn_stored.at(16 * NG))
            pool.wait_ge(*s.idx_ready.at(1))
            fetch(0)
            fetch(1)
            for e in range(E):
                if e + 2 < E:
                    pool.wait_ge(*s.eT_full.at(e + 1))
                    fetch(e + 2)
                deliver(e)

        @block.sync
        def _(sp):
            def load_weights(j, par):
                e = 2 * j + par
                if not (isinstance(j, int) and j < 1):
                    sp.wait_ge(*s.y_full.at(e - 1))
                sp.dma_start(k.w1[:, par, :], w.w1[bass.ds(e * C, C), :]).then_inc(s.w1_landed[par].h, 16)
                sp.dma_start(k.w2[:, par, :, :], w.w2[bass.ds(e * FH, FH), :].rearrange("(f p) c -> p f c", p=P))\
                    .then_inc(s.w2_landed[par].h, 16)

            def store_rows(i):
                sp.wait_ge(*s.gx_ready.at(i + 1))
                sp.dma_start(k.xn_dram[i * S:(i + 1) * S, :].rearrange("(t p) c -> p t c", p=P),
                             k.xn[:, i * S:(i + 1) * S].rearrange("p (t c) -> p t c", c=C)).then_inc(s.xn_stored.h, 16)

            def load_results(i):
                for c in range(2):
                    sp.dma_start(k.rows_back[:, c, i * TB:(i + 1) * TB, :], k.y_rows[c * T + i * S:c * T + (i + 1) * S, :]
                                 .rearrange("(t p) c -> p t c", p=P)).then_inc(s.gathered[i].h, 16)

            for i in range(NG):
                store_rows(i)
            for e in range(E):
                load_weights(e // 2, e % 2)
            for par in range(2):
                sp.wait_ge(*s.y_stored[par].at(16 * ST * PAIRS))
            for i in range(NG):
                load_results(i)

    counts = {
        s.ln_stats: B, s.ln_step: 2, s.ln_var: 1, s.ln_std: 1, s.ln_rstd: 1, s.gx_ready: NG, s.gT_full: NG, s.gT_free: NG, s.gl_full: NG,
        s.gl_free: NG, s.choice_ready: 2, s.diff_ready: 2, s.exp_ready: 2, s.rank_full: 2,
        s.rt_step: k.route_steps, s.idx_ready: 1, s.marks_ready: 2, s.inv_full: 1, s.xn_stored: 16 * NG, s.eT_full: E, s.eT_free: E,
        s.h_full: FC * E, s.act_done: FC * E, s.y_full: E, s.y_ready: E, s.combined: 2 * NG,
    }
    if w.ln_w is not None:
        counts[s.ga_step] = 2 * NG
    for group in (s.w1_landed, s.w2_landed):
        counts |= {x: 16 * PAIRS for x in group}
    for group in (s.xe_landed, s.y_stored):
        counts |= {x: 16 * ST * PAIRS for x in group}
    counts |= {x: 16 * 2 for x in s.gathered}
    for signal, n in counts.items():
        signal.base += n


class Signals:

    def __init__(self, new):
        self.ln_stats = new("ln_stats")
        self.ln_step = new("ln_step")
        self.ln_var = new("ln_var")
        self.ln_std = new("ln_std")
        self.ln_rstd = new("ln_rstd")
        self.xa_ready = new("xa_ready")
        self.xT_full, self.xT_free = new("xT_full"), new("xT_free")
        self.q_full, self.q_free = new("q_full"), new("q_free")
        self.k_full, self.k_free = new("k_full"), new("k_free")
        self.v_full, self.v_free = new("v_full"), new("v_free")
        self.cT_full, self.cT_free = new("cT_full"), new("cT_free")
        self.out_full, self.out_free = new("out_full"), new("out_free")
        self.res_done = new("res_done")
        self.cv_step = new("cv_step")
        self.xd_ready = new("xd_ready")
        self.sp_hi, self.sp_rest, self.sp_mid = new("sp_hi"), new("sp_rest"), new("sp_mid")
        self.pq_ready = new("pq_ready")
        self.parts_written = new("parts_written")
        self.mT_full, self.mT_free = new("mT_full"), new("mT_free")
        self.oT_full, self.oT_free = new("oT_full"), new("oT_free")
        self.nm_step = new("nm_step")
        self.nm_ready = new("nm_ready")
        self.pv_done = new("pv_done")
        self.o_free = new("o_free")
        self.rec_done = new("rec_done")
        self.vs_ready = new("vs_ready")
        self.qk_landed = [new(f"qk_landed{g}") for g in range(G)]
        self.m_landed = [new(f"m_landed{g}") for g in range(G)]
        self.max_full, self.max_taken = new("max_full"), new("max_taken")
        self.sc_full, self.pt_ready = new("sc_full"), new("pt_ready")
        self.gx_ready = new("gx_ready")
        self.ga_step = new("ga_step")
        self.gT_full, self.gT_free = new("gT_full"), new("gT_free")
        self.gl_full, self.gl_free = new("gl_full"), new("gl_free")
        self.choice_ready = new("choice_ready")
        self.diff_ready, self.exp_ready = new("diff_ready"), new("exp_ready")
        self.rank_full = new("rank_full")
        self.rt_step = new("rt_step")
        self.marks_ready = new("marks_ready")
        self.inv_full = new("inv_full")
        self.idx_ready = new("idx_ready")
        self.xn_stored = new("xn_stored")
        self.xe_landed = [new(f"xe_landed{i}") for i in range(2)]
        self.w1_landed = [new(f"w1_landed{i}") for i in range(2)]
        self.w2_landed = [new(f"w2_landed{i}") for i in range(2)]
        self.eT_full, self.eT_free = new("eT_full"), new("eT_free")
        self.h_full, self.act_done = new("h_full"), new("act_done")
        self.y_full, self.y_ready = new("y_full"), new("y_ready")
        self.y_stored = [new(f"y_stored{i}") for i in range(2)]
        self.gathered = [new(f"gathered{i}") for i in range(NT // TB)]
        self.combined = new("combined")


class Buffers:
    pass


STAGES = ("moe0", "attn0", "moe0", "attn1f", "moe1", "attn1", "attn1f", "moe1")


def program(nc, a, out):
    ctx = ExitStack()
    with ctx:
        def sb(name, shape, dt=F32):
            return ctx.enter_context(nc.sbuf_tensor(name, [P] + shape, dt))

        k = Buffers()
        k.sig = Signals(lambda name: Signal(ctx.enter_context(nc.semaphore(name))))
        s_in = ctx.enter_context(nc.semaphore("inputs_landed"))
        k.zeroed = ctx.enter_context(nc.semaphore("y_rows_zeroed"))
        s_xn = ctx.enter_context(nc.semaphore("xn_zeroed"))
        s_vs = ctx.enter_context(nc.semaphore("vs_zeroed"))
        s_down = ctx.enter_context(nc.semaphore("down_made"))
        s_fill = ctx.enter_context(nc.semaphore("const_filled"))
        s_cast = ctx.enter_context(nc.semaphore("const_cast"))
        s_out = ctx.enter_context(nc.semaphore("stored"))

        x, hid = sb("x", [T * C // P]), sb("hid", [T * C // P])
        k.xn = sb("xn", [T * C // P])
        k.PS = ctx.enter_context(nc.psum_tensor("PS", [P, 8, 512], F32))
        k.ident, k.identb = sb("ident", [P]), sb("identb", [P], BF16)
        k.mask_q, k.mask_k = sb("mask_q", [P], BF16), sb("mask_k", [P], BF16)
        k.tri, k.onesb, k.ones_t = sb("tri", [P], BF16), sb("onesb", [P], BF16), sb("ones_t", [NT])
        down_i = sb("down_i", [16], I32)
        down8, down16 = sb("down8", [8]), sb("down16", [16])
        k.xa, k.st, k.eps = sb("xa", [TB, C]), sb("st", [NT * 6]), sb("eps", [1])
        k.mean, k.dev, k.std, k.rstd, k.rstd2 = (sb(n, [NT]) for n in ("mean", "dev", "std", "rstd", "rstd2"))
        k.xnT = sb("xnT", [S + 2])
        k.xdT = sb("xdT", [S // 2])[:, :]
        k.cv = sb("cv", [2, S // 2])
        k.q32, k.k32 = sb("q32", [S])[:, :], sb("k32", [S])
        k.rest = sb("rest", [S])
        k.parts = sb("parts", [2, 3, S], BF16)
        k.vst = sb("vst", [TB, C])
        k.vs = sb("vs", [G, TB, HG, 32])
        k.qa, k.ka = sb("qa", [G, HG, S], BF16), sb("ka", [G, HG, S], BF16)
        k.mx = sb("mx", [2, 16])
        k.nm32 = sb("nm32", [2, P])[0:16]
        k.nm = sb("nm", [2, 3, P], BF16)[0:16]
        k.osb = sb("osb", [S])[:, :]
        k.rec = sb("rec", [TB, HG])
        k.ctx, k.tmp = sb("ctx", [TB, C]), sb("tmp", [TB, C])
        k.ctxT = sb("ctxT", [S])[:, :]
        k.pt = sb("pt", [2, 5120])
        k.at_rank = k.pt[:, :, :].bitcast(BF16)[:, :, 0:NT * P]
        k.rows_back = k.pt[:, :, 0:NT * C].rearrange("p c (t d) -> p c t d", d=C)
        k.logits, k.ra, k.rb, k.rc, k.rd = (sb(f"r{i}", [NT * 16]) for i in range(5))
        k.onehot = sb("onehot", [2, NT * 16], BF16)
        k.rv, k.before, k.idx = sb("rv", [10, NT]), sb("before", [16]), sb("idx", [2, 64], I32)
        k.count, k.lane, k.row_high = sb("count", [P]), sb("lane", [1]), sb("row_high", [2, NT], BF16)
        count_i, lane_i, high_i = sb("count_i", [P], I32), sb("lane_i", [1], I32), sb("high_i", [2 * NT], I32)
        k.in_tile = k.xn[:, :].bitcast(BF16).rearrange("p (c n) -> p c n", c=2)
        part = lambda i, n=1: k.pt[:, :, i * S:(i + n) * S]
        k.hT = part(0, FC).rearrange("p e (f n) -> p e f n", f=FC)
        k.w2 = part(4).rearrange("p e (f c) -> p e f c", f=FC)
        k.xe, k.ys = (part(i).rearrange("p e (t c) -> p e t c", c=C) for i in (5, 6))
        k.xeT, k.w1 = part(7), part(8)
        k.q_dram = nc.dram_tensor("q_parts", (NPROD, D, H, S), BF16).ap()
        k.k_dram = nc.dram_tensor("k_parts", (NPROD, D, H, S), BF16).ap()
        ROWS_Y = 2 * T
        k.xn_dram = nc.dram_tensor("xn_rows", (T, C), F32).ap()
        k.y_rows = nc.dram_tensor("y_rows", (ROWS_Y, C), F32).ap()

        loads = [(x[:, :].rearrange("p (t c) -> p t c", c=C), a["x"].rearrange("b (t p) c -> p (b t) c", p=P))]

        def weight(name, src, n=C):
            tile = sb(name, [n])
            loads.append((tile[:, :], src))
            return tile[:, :]

        def rows_of(v):
            return v.partition_broadcast(P)

        def column(v):
            return v.rearrange("(p o) -> p o", o=1)

        def attention_weights(tag, q, kk, v, o, qb, kb, vb, ob, ln_w=None, ln_b=None, conv_w=None, conv_b=None):
            m = Buffers()
            m.wq, m.wk = weight(tag + "wq", q), weight(tag + "wk", kk)
            m.wv, m.wo = weight(tag + "wv", v), weight(tag + "wo", o)
            m.qb, m.kb = weight(tag + "qb", column(qb), 1), weight(tag + "kb", column(kb), 1)
            m.vb, m.ob = weight(tag + "vb", rows_of(vb)), weight(tag + "ob", rows_of(ob))
            m.ln_w = m.ln_b = m.conv_w = m.conv_b = None
            if ln_w is not None:
                m.ln_w, m.ln_b = weight(tag + "lw", column(ln_w), 1), weight(tag + "lb", column(ln_b), 1)
            if conv_w is not None:
                m.conv_w, m.conv_b = weight(tag + "cw", conv_w, 3), weight(tag + "cb", column(conv_b), 1)
            return m

        attn0 = attention_weights("a0", a["a0_qw"], a["a0_kw"], a["a0_vw"], a["a0_ow"], a["a0_qb"], a["a0_kb"],
                                  a["a0_vb"], a["a0_ob"], conv_w=a["a0_cw"], conv_b=a["a0_cb"])
        w3, b3 = a["a1_w"], a["a1_b"]
        attn1 = attention_weights("a1", w3[:, 0:C], w3[:, C:2 * C], w3[:, 2 * C:3 * C], a["a1_ow"], b3[0:C],
                                  b3[C:2 * C], b3[2 * C:3 * C], a["a1_ob"])
        attn1f = attention_weights("af", a["f1_qw"], a["f1_kw"], a["f1_vw"], a["f1_ow"], a["f1_qb"], a["f1_kb"],
                                   a["f1_vb"], a["f1_ob"], ln_w=a["f1_l1w"], ln_b=a["f1_l1b"])
        def expert_weights(tag, g, w1, b1, w2, b2, E, down):
            m = Buffers()
            m.wg = weight(tag + "g", g, E)
            m.w1, m.w2 = w1.rearrange("e c f -> (e c) f"), w2.rearrange("e f c -> (e f) c")
            m.b1 = weight(tag + "b1", b1, E * FC)
            m.b2 = weight(tag + "b2", rows_of(b2.rearrange("e c -> (e c)")), E * C)
            m.ln_w = m.ln_b = None
            m.down = down
            return m

        ffn0 = expert_weights("f0", a["f0_g"], a["f0_w1"], a["f0_b1"], a["f0_w2"], a["f0_b2"], 8, down8[:, :])
        ffn0.gelu_tanh, ffn0.counted = True, 256
        ffn1 = expert_weights("f1", a["f1_g"], a["f1_w1"], a["f1_b1"], a["f1_w2"], a["f1_b2"], 16, down16[:, :])
        ffn1.gelu_tanh, ffn1.counted = False, T
        ffn1.ln_w, ffn1.ln_b = weight("l2w", rows_of(a["f1_l2w"])), weight("l2b", rows_of(a["f1_l2b"]))

        with nc.Block() as block:
            @block.sync
            def _(sp):
                for tile, source in loads:
                    sp.dma_start(tile, source).then_inc(s_in, 16)
                sp.wait_ge(s_xn, 1)
                for half in range(2):
                    n = ROWS_Y // 2
                    sp.dma_start(k.y_rows[half * n:(half + 1) * n, :].rearrange("(p r) c -> p (r c)", p=P),
                                 k.xn[:, :]).then_inc(k.zeroed, 16)
                sp.wait_ge(s_in, 16 * len(loads))

            @block.vector
            def _(dve):
                nc.vector.memset(k.xn[:, :], 0.0).then_inc(s_xn, 1)
                nc.vector.memset(k.qa[:, :, :, :], 0.0)
                nc.vector.memset(k.ka[:, :, :, :], 0.0).then_inc(s_cast, 1)
                nc.vector.memset(k.onesb[:, :], 1.0)
                nc.vector.memset(k.ones_t[:, :], 1.0)
                nc.vector.memset(k.eps[:, :], EPS)
                nc.vector.memset(k.xnT[:, 0:1], 0.0)
                dve.wait_ge(s_cast, 1)
                dve.wait_ge(s_vs, 1)
                nc.vector.memset(k.ka[64:96, :, :, :], 1.0)
                nc.vector.memset(k.vs[:, :, :, :, D:D + 1], 1.0)
                dve.wait_ge(s_down, 2)
                nc.vector.tensor_copy(k.count[:, :], count_i[:, :])
                nc.vector.tensor_copy(k.lane[:, :], lane_i[:, :])
                nc.vector.tensor_copy(k.row_high[:, :, :].rearrange("p c t -> p (c t)"), high_i[:, :])
                nc.vector.tensor_copy(down16[:, :], down_i[:, :])
                nc.vector.tensor_scalar(down8[:, :], down_i[:, 0:8], -8.0, None, ALU.add)

            @block.gpsimd
            def _(pool):
                pool.iota(down_i[:, :], pattern=[[-1, 16]], base=16, channel_multiplier=0).then_inc(s_down, 1)
                pool.iota(count_i[:, :], pattern=[[1, P]], base=0, channel_multiplier=0)
                pool.iota(lane_i[:, :], pattern=[[0, 1]], base=0, channel_multiplier=1)
                pool.iota(high_i[:, :], pattern=[[P, 2 * NT]], base=-2 * T, channel_multiplier=0).then_inc(s_down, 1)
                pool.memset(k.vs[:, :, :, :, :], 0.0).then_inc(s_vs, 1)
                pool.memset(k.ident[:, :], 0.0)
                pool.memset(k.identb[:, :], 0.0)
                pool.memset(k.mask_q[:, :], 0.0)
                pool.memset(k.mask_k[:, :], 0.0)
                pool.memset(k.tri[:, :], 1.0).then_inc(s_fill, 1)
                pool.wait_ge(s_fill, 1)
                for m in (k.ident, k.identb):
                    pool.affine_select(out=m[:, :], in_=m[:, :], compare_op=ALU.not_equal, fill=1.0, base=0,
                                       pattern=[[-1, P]], channel_multiplier=1)
                pool.affine_select(out=k.mask_q[:, :], in_=k.mask_q[:, :], compare_op=ALU.is_ge, fill=MASKED, base=0,
                                   pattern=[[-1, P]], channel_multiplier=1)
                pool.affine_select(out=k.mask_k[:, :], in_=k.mask_k[:, :], compare_op=ALU.is_ge, fill=MASKED, base=0,
                                   pattern=[[1, P]], channel_multiplier=-1)
                pool.affine_select(out=k.tri[:, :], in_=k.tri[:, :], compare_op=ALU.is_gt, fill=0.0, base=0,
                                   pattern=[[1, P]], channel_multiplier=-1)

        for stage in STAGES:
            if stage == "moe0":
                moe(nc, k, ffn0, x, x, 8, 256, 0.5, ("add", 1e-9), 0.0)
            elif stage == "attn0":
                attention(nc, k, attn0, x, x, False)
            elif stage == "attn1f":
                attention(nc, k, attn1f, x, hid, True, twice=True)
            elif stage == "moe1":
                moe(nc, k, ffn1, hid, x, 16, 2 * T // 16, 0.5 * 0.8, ("max", 1.1920929e-07), 0.5)
            elif stage == "attn1":
                attention(nc, k, attn1, x, x, True)

        with nc.Block() as block:
            @block.sync
            def _(sp):
                sp.dma_start(out.rearrange("b (t p) c -> p (b t) c", p=P),
                             x[:, :].rearrange("p (t c) -> p t c", c=C)).then_inc(s_out, 16)
                sp.wait_ge(s_out, 16)


def layout(np, i):
    t = lambda n: np.ascontiguousarray(i[n].T)
    b1 = lambda n: np.ascontiguousarray(i[n].reshape(-1, FC, P).transpose(2, 0, 1).reshape(P, -1))
    return {
        "x": i["L0_attn_x"],
        "a0_qw": t("L0_attn_q_w"), "a0_kw": t("L0_attn_k_w"), "a0_vw": t("L0_attn_v_w"), "a0_ow": t("L0_attn_out_w"),
        "a0_qb": i["L0_attn_q_b"], "a0_kb": i["L0_attn_k_b"], "a0_vb": i["L0_attn_v_b"], "a0_ob": i["L0_attn_out_b"],
        "a0_cw": i["L0_attn_conv_w"].reshape(C, 3), "a0_cb": i["L0_attn_conv_b"],
        "f0_g": i["L0_ffn_Wg"], "f0_w1": i["L0_ffn_W1"], "f0_b1": b1("L0_ffn_b1"), "f0_w2": i["L0_ffn_W2"],
        "f0_b2": i["L0_ffn_b2"],
        "a1_w": t("L1_attn_qkv_w"), "a1_b": i["L1_attn_qkv_b"], "a1_ow": t("L1_attn_out_w"), "a1_ob": i["L1_attn_out_b"],
        "f1_l1w": i["L1_ffn_ln1_w"], "f1_l1b": i["L1_ffn_ln1_b"],
        "f1_qw": i["L1_ffn_q_w"], "f1_kw": i["L1_ffn_k_w"], "f1_vw": i["L1_ffn_v_w"], "f1_ow": i["L1_ffn_o_w"],
        "f1_qb": i["L1_ffn_q_b"], "f1_kb": i["L1_ffn_k_b"], "f1_vb": i["L1_ffn_v_b"], "f1_ob": i["L1_ffn_o_b"],
        "f1_l2w": i["L1_ffn_ln2_w"], "f1_l2b": i["L1_ffn_ln2_b"], "f1_g": i["L1_ffn_router_w"],
        "f1_w1": i["L1_ffn_fc1_w"], "f1_b1": b1("L1_ffn_fc1_b"), "f1_w2": i["L1_ffn_fc2_w"], "f1_b2": i["L1_ffn_fc2_b"],
    }


def kernel(**inputs):
    import numpy as np
    import concourse.bacc as bacc
    from concourse.bass_utils import run_bass_kernel_spmd

    nc = bacc.Bacc("TRN2", target_bir_lowering=False, num_devices=1)
    arrays, args = {}, {}
    for name, array in layout(np, {n: np.asarray(v) for n, v in inputs.items()}).items():
        array = np.ascontiguousarray(array)
        arrays[f"in_{name}"] = array
        args[name] = nc.dram_tensor(f"in_{name}", array.shape, mybir.dt.from_np(array.dtype), kind="ExternalInput").ap()
    out = nc.dram_tensor("out", (B, S, C), F32, kind="ExternalOutput").ap()
    program(nc, args, out)
    r = run_bass_kernel_spmd(nc, [arrays], core_ids=[0])
    return r.results[0]["out"]
```
